# Optimizing a Trainium2 kernel written in Bass

```python
import numpy as np
import jax
import jax.numpy as jnp

def _softmax(x, axis=-1):
    return jax.nn.softmax(x, axis=axis)

def _gelu(x):
    return jax.nn.gelu(x, approximate=True)

def _silu(x):
    return jax.nn.silu(x)

def _sigmoid(x):
    return jax.nn.sigmoid(x)

def _layernorm(x, axis=-1, eps=1e-05):
    m = jnp.mean(x, axis=axis, keepdims=True)
    v = jnp.var(x, axis=axis, keepdims=True)
    return (x - m) / jnp.sqrt(v + eps)

def _scatter_add(tgt, idx, src, axis=0):
    return tgt.at[idx].add(src)

def _segment_sum(src, seg, n):
    return jax.ops.segment_sum(src, seg, n)
kernel_name = 'mk_xattn_seq_d2_seqx_r4_2279ee'

def setup_inputs(seed: int=0):
    np.random.seed(seed)
    _w = jnp.asarray

    def _rec_inputs():
        import jax
        import jax.numpy as jnp
        _rk = jax.random.key(seed)
        x = -0.0002928 + 1 * jax.random.normal(jax.random.fold_in(_rk, 1), (64, 256, 256), jnp.float32)
        _lenS = 256 - jax.random.randint(jax.random.fold_in(_rk, 7), (64,), 0, max(1, 256 // 4) + 1, jnp.int32)
        _lenS2 = 120 - jax.random.randint(jax.random.fold_in(_rk, 8), (64,), 0, max(1, 120 // 4) + 1, jnp.int32)
        _ctx_1024P = jax.random.normal(jax.random.fold_in(_rk, 11), (64, 16, 256), jnp.float32)
        _ctx_1024c = jax.random.dirichlet(jax.random.fold_in(_rk, 511), 0.3 * jnp.ones((16,), jnp.float32), (64, 120))
        _ctx_1024t = jnp.einsum('bsk,bkd->bsd', _ctx_1024c, _ctx_1024P)
        _ctx_1024t = _ctx_1024t * jax.lax.rsqrt(jnp.mean(jnp.square(_ctx_1024t)) + 1e-12) * 0.953939
        ctx_1024 = -1.39393e-06 + 0.999914 * (_ctx_1024t + 0.3 * jax.random.normal(jax.random.fold_in(_rk, 611), (64, 120, 256), jnp.float32))
        _validS = jnp.arange(256)[None, :] < _lenS[:, None]
        _validS2 = jnp.arange(120)[None, :] < _lenS2[:, None]
        _causal = jnp.tril(jnp.ones((256, 256), dtype=bool))
        mask_BxSxS2_bk0 = jnp.logical_not(jnp.broadcast_to(_validS2[:, None, :], (64, 256, 120)))
        return (x, ctx_1024, mask_BxSxS2_bk0)
    x, ctx_1024, mask_BxSxS2_bk0 = _rec_inputs()

    def _L0_xattn_setup():
        import jax, jax.numpy as jnp
        import numpy as np
        B, S, D, H, FF = (2, 512, 256, 16, 1024)
        DK = D // H
        LN_EPS = 1e-05

        def layer_norm(x, g, b):
            mu = jnp.mean(x, axis=-1, keepdims=True)
            var = jnp.var(x, axis=-1, keepdims=True)
            return (x - mu) * jax.lax.rsqrt(var + LN_EPS) * g + b

        def split_heads(t):
            b, l, _ = t.shape
            return t.reshape(b, l, H, DK).transpose(0, 2, 1, 3)

        def mha(q_in, k_in, v_in, wq, wk, wv, wo, causal):
            q = split_heads(q_in @ wq)
            k = split_heads(k_in @ wk)
            v = split_heads(v_in @ wv)
            attn = jnp.einsum('bhqd,bhkd->bhqk', q, k) * DK ** (-0.5)
            if causal:
                lq = q.shape[2]
                mask = jnp.tril(jnp.ones((lq, lq), dtype=bool))
                attn = jnp.where(mask, attn, -jnp.inf)
            attn = jax.nn.softmax(attn, axis=-1)
            out = jnp.einsum('bhqk,bhkd->bhqd', attn, v)
            out = out.transpose(0, 2, 1, 3).reshape(q_in.shape[0], q_in.shape[1], D)
            return out @ wo
        key = jax.random.key(seed)
        ks = jax.random.split(key, 16)
        s = 1.0 / np.sqrt(D)
        inp = {'x': jax.random.normal(ks[0], (B, S, D), jnp.float32), 'encoder_output': jax.random.normal(ks[1], (B, S, D), jnp.float32), 'sa_wq': jax.random.normal(ks[2], (D, D), jnp.float32) * s, 'sa_wk': jax.random.normal(ks[3], (D, D), jnp.float32) * s, 'sa_wv': jax.random.normal(ks[4], (D, D), jnp.float32) * s, 'sa_wo': jax.random.normal(ks[5], (D, D), jnp.float32) * s, 'ca_wq': jax.random.normal(ks[6], (D, D), jnp.float32) * s, 'ca_wk': jax.random.normal(ks[7], (D, D), jnp.float32) * s, 'ca_wv': jax.random.normal(ks[8], (D, D), jnp.float32) * s, 'ca_wo': jax.random.normal(ks[9], (D, D), jnp.float32) * s, 'ffn_w1': jax.random.normal(ks[10], (D, FF), jnp.float32) * s, 'ffn_b1': jnp.zeros((FF,), jnp.float32), 'ffn_w2': jax.random.normal(ks[11], (FF, D), jnp.float32) * (1.0 / np.sqrt(FF)), 'ffn_b2': jnp.zeros((D,), jnp.float32), 'ln1_g': jnp.ones((D,), jnp.float32), 'ln1_b': jnp.zeros((D,), jnp.float32), 'ln2_g': jnp.ones((D,), jnp.float32), 'ln2_b': jnp.zeros((D,), jnp.float32), 'ln3_g': jnp.ones((D,), jnp.float32), 'ln3_b': jnp.zeros((D,), jnp.float32)}
        return inp
    _L0_xattn_all = _L0_xattn_setup()
    _L0_xattn_in = {k: v for k, v in _L0_xattn_all.items() if k in ('sa_wq', 'sa_wk', 'sa_wv', 'sa_wo', 'ca_wq', 'ca_wk', 'ca_wv', 'ca_wo', 'ffn_w1', 'ffn_b1', 'ffn_w2', 'ffn_b2', 'ln1_g', 'ln1_b', 'ln2_g', 'ln2_b', 'ln3_g', 'ln3_b')}
    del _L0_xattn_all

    def _L1_xattn_setup():
        import jax, jax.numpy as jnp
        import numpy as np
        EPS = 1e-05

        def layer_norm(x, w, b):
            mu = jnp.mean(x, axis=-1, keepdims=True)
            var = jnp.var(x, axis=-1, keepdims=True)
            return (x - mu) * jax.lax.rsqrt(var + EPS) * w + b
        key = jax.random.key(seed)
        ks = jax.random.split(key, 12)
        B, N, M, C = (2, 512, 512, 256)
        H = 16
        hid = 4 * C
        s = lambda d: 1.0 / np.sqrt(d)
        return {'x': jax.random.normal(ks[0], (B, N, C), jnp.float32), 'context': jax.random.normal(ks[1], (B, M, C), jnp.float32), 'xa_mask': jax.random.bernoulli(ks[2], 0.1, (B, N, M)), 'qn_w': jnp.ones((C,), jnp.float32), 'qn_b': jnp.zeros((C,), jnp.float32), 'cn_w': jnp.ones((C,), jnp.float32), 'cn_b': jnp.zeros((C,), jnp.float32), 'n2_w': jnp.ones((C,), jnp.float32), 'n2_b': jnp.zeros((C,), jnp.float32), 'q_w': jax.random.normal(ks[3], (C, C), jnp.float32) * s(C), 'kv_w': jax.random.normal(ks[4], (C, 2 * C), jnp.float32) * s(C), 'proj_w': jax.random.normal(ks[5], (C, C), jnp.float32) * s(C), 'proj_b': jnp.zeros((C,), jnp.float32), 'fc1_w': jax.random.normal(ks[6], (C, hid), jnp.float32) * s(C), 'fc1_b': jnp.zeros((hid,), jnp.float32), 'fc2_w': jax.random.normal(ks[7], (hid, C), jnp.float32) * s(hid), 'fc2_b': jnp.zeros((C,), jnp.float32)}
    _L1_xattn_all = _L1_xattn_setup()
    _L1_xattn_in = {k: v for k, v in _L1_xattn_all.items() if k in ('qn_w', 'qn_b', 'cn_w', 'cn_b', 'n2_w', 'n2_b', 'q_w', 'kv_w', 'proj_w', 'proj_b', 'fc1_w', 'fc1_b', 'fc2_w', 'fc2_b')}
    del _L1_xattn_all
    return {'x': x, 'ctx_1024': ctx_1024, 'mask_BxSxS2_bk0': mask_BxSxS2_bk0, 'L0_xattn_sa_wq': _L0_xattn_in['sa_wq'], 'L0_xattn_sa_wk': _L0_xattn_in['sa_wk'], 'L0_xattn_sa_wv': _L0_xattn_in['sa_wv'], 'L0_xattn_sa_wo': _L0_xattn_in['sa_wo'], 'L0_xattn_ca_wq': _L0_xattn_in['ca_wq'], 'L0_xattn_ca_wk': _L0_xattn_in['ca_wk'], 'L0_xattn_ca_wv': _L0_xattn_in['ca_wv'], 'L0_xattn_ca_wo': _L0_xattn_in['ca_wo'], 'L0_xattn_ffn_w1': _L0_xattn_in['ffn_w1'], 'L0_xattn_ffn_b1': _L0_xattn_in['ffn_b1'], 'L0_xattn_ffn_w2': _L0_xattn_in['ffn_w2'], 'L0_xattn_ffn_b2': _L0_xattn_in['ffn_b2'], 'L0_xattn_ln1_g': _L0_xattn_in['ln1_g'], 'L0_xattn_ln1_b': _L0_xattn_in['ln1_b'], 'L0_xattn_ln2_g': _L0_xattn_in['ln2_g'], 'L0_xattn_ln2_b': _L0_xattn_in['ln2_b'], 'L0_xattn_ln3_g': _L0_xattn_in['ln3_g'], 'L0_xattn_ln3_b': _L0_xattn_in['ln3_b'], 'L1_xattn_qn_w': _L1_xattn_in['qn_w'], 'L1_xattn_qn_b': _L1_xattn_in['qn_b'], 'L1_xattn_cn_w': _L1_xattn_in['cn_w'], 'L1_xattn_cn_b': _L1_xattn_in['cn_b'], 'L1_xattn_n2_w': _L1_xattn_in['n2_w'], 'L1_xattn_n2_b': _L1_xattn_in['n2_b'], 'L1_xattn_q_w': _L1_xattn_in['q_w'], 'L1_xattn_kv_w': _L1_xattn_in['kv_w'], 'L1_xattn_proj_w': _L1_xattn_in['proj_w'], 'L1_xattn_proj_b': _L1_xattn_in['proj_b'], 'L1_xattn_fc1_w': _L1_xattn_in['fc1_w'], 'L1_xattn_fc1_b': _L1_xattn_in['fc1_b'], 'L1_xattn_fc2_w': _L1_xattn_in['fc2_w'], 'L1_xattn_fc2_b': _L1_xattn_in['fc2_b']}

def reference(x, ctx_1024, mask_BxSxS2_bk0, L0_xattn_sa_wq, L0_xattn_sa_wk, L0_xattn_sa_wv, L0_xattn_sa_wo, L0_xattn_ca_wq, L0_xattn_ca_wk, L0_xattn_ca_wv, L0_xattn_ca_wo, L0_xattn_ffn_w1, L0_xattn_ffn_b1, L0_xattn_ffn_w2, L0_xattn_ffn_b2, L0_xattn_ln1_g, L0_xattn_ln1_b, L0_xattn_ln2_g, L0_xattn_ln2_b, L0_xattn_ln3_g, L0_xattn_ln3_b, L1_xattn_qn_w, L1_xattn_qn_b, L1_xattn_cn_w, L1_xattn_cn_b, L1_xattn_n2_w, L1_xattn_n2_b, L1_xattn_q_w, L1_xattn_kv_w, L1_xattn_proj_w, L1_xattn_proj_b, L1_xattn_fc1_w, L1_xattn_fc1_b, L1_xattn_fc2_w, L1_xattn_fc2_b):
    import jax
    import jax.numpy as jnp

    def _L0_xattn_ref(x, encoder_output, sa_wq, sa_wk, sa_wv, sa_wo, ca_wq, ca_wk, ca_wv, ca_wo, ffn_w1, ffn_b1, ffn_w2, ffn_b2, ln1_g, ln1_b, ln2_g, ln2_b, ln3_g, ln3_b):
        import jax, jax.numpy as jnp
        import numpy as np
        B, S, D, H, FF = (2, 512, 256, 16, 1024)
        DK = D // H
        LN_EPS = 1e-05

        def layer_norm(x, g, b):
            mu = jnp.mean(x, axis=-1, keepdims=True)
            var = jnp.var(x, axis=-1, keepdims=True)
            return (x - mu) * jax.lax.rsqrt(var + LN_EPS) * g + b

        def split_heads(t):
            b, l, _ = t.shape
            return t.reshape(b, l, H, DK).transpose(0, 2, 1, 3)

        def mha(q_in, k_in, v_in, wq, wk, wv, wo, causal):
            q = split_heads(q_in @ wq)
            k = split_heads(k_in @ wk)
            v = split_heads(v_in @ wv)
            attn = jnp.einsum('bhqd,bhkd->bhqk', q, k) * DK ** (-0.5)
            if causal:
                lq = q.shape[2]
                mask = jnp.tril(jnp.ones((lq, lq), dtype=bool))
                attn = jnp.where(mask, attn, -jnp.inf)
            attn = jax.nn.softmax(attn, axis=-1)
            out = jnp.einsum('bhqk,bhkd->bhqd', attn, v)
            out = out.transpose(0, 2, 1, 3).reshape(q_in.shape[0], q_in.shape[1], D)
            return out @ wo
        h = layer_norm(x, ln1_g, ln1_b)
        x = x + mha(h, h, h, sa_wq, sa_wk, sa_wv, sa_wo, causal=True)
        h = layer_norm(x, ln2_g, ln2_b)
        x = x + mha(h, encoder_output, encoder_output, ca_wq, ca_wk, ca_wv, ca_wo, causal=False)
        h = layer_norm(x, ln3_g, ln3_b)
        x = x + (jax.nn.relu(h @ ffn_w1 + ffn_b1) @ ffn_w2 + ffn_b2)
        return x

    def _L1_xattn_ref(x, context, xa_mask, qn_w, qn_b, cn_w, cn_b, n2_w, n2_b, q_w, kv_w, proj_w, proj_b, fc1_w, fc1_b, fc2_w, fc2_b):
        import jax, jax.numpy as jnp
        import numpy as np
        EPS = 1e-05

        def layer_norm(x, w, b):
            mu = jnp.mean(x, axis=-1, keepdims=True)
            var = jnp.var(x, axis=-1, keepdims=True)
            return (x - mu) * jax.lax.rsqrt(var + EPS) * w + b
        B, N, C = x.shape
        M = context.shape[1]
        H = 16
        D = C // H
        scale = D ** (-0.5)
        xq = layer_norm(x, qn_w, qn_b)
        ctx = layer_norm(context, cn_w, cn_b)
        q = (xq @ q_w).reshape(B, N, H, D)
        kv = (ctx @ kv_w).reshape(B, M, 2, H, D)
        k, v = (kv[:, :, 0], kv[:, :, 1])
        attn = jnp.einsum('bnhd,bmhd->bhnm', q, k) * scale
        neg = -jnp.finfo(attn.dtype).max
        attn = jnp.where(xa_mask[:, None, :, :], neg, attn)
        attn = jax.nn.softmax(attn, axis=-1)
        out = jnp.einsum('bhnm,bmhd->bnhd', attn, v).reshape(B, N, C)
        out = out @ proj_w + proj_b
        x = x + out
        h = layer_norm(x, n2_w, n2_b)
        h = jax.nn.gelu(h @ fc1_w + fc1_b, approximate=False) @ fc2_w + fc2_b
        return x + h
    x = _L0_xattn_ref(x, ctx_1024, L0_xattn_sa_wq, L0_xattn_sa_wk, L0_xattn_sa_wv, L0_xattn_sa_wo, L0_xattn_ca_wq, L0_xattn_ca_wk, L0_xattn_ca_wv, L0_xattn_ca_wo, L0_xattn_ffn_w1, L0_xattn_ffn_b1, L0_xattn_ffn_w2, L0_xattn_ffn_b2, L0_xattn_ln1_g, L0_xattn_ln1_b, L0_xattn_ln2_g, L0_xattn_ln2_b, L0_xattn_ln3_g, L0_xattn_ln3_b)
    x = _L1_xattn_ref(x, ctx_1024, mask_BxSxS2_bk0, L1_xattn_qn_w, L1_xattn_qn_b, L1_xattn_cn_w, L1_xattn_cn_b, L1_xattn_n2_w, L1_xattn_n2_b, L1_xattn_q_w, L1_xattn_kv_w, L1_xattn_proj_w, L1_xattn_proj_b, L1_xattn_fc1_w, L1_xattn_fc1_b, L1_xattn_fc2_w, L1_xattn_fc2_b)
    return x

_drawn_inputs = setup_inputs


def setup_inputs(seed=0):
    import zlib

    import numpy as np

    out = dict(_drawn_inputs(seed))
    spreads = {'L0_xattn_ffn_b1': (0.0, 0.1),
     'L0_xattn_ffn_b2': (0.0, 0.1),
     'L0_xattn_ln1_g': (1.0, 0.2),
     'L0_xattn_ln1_b': (0.0, 0.1),
     'L0_xattn_ln2_g': (1.0, 0.2),
     'L0_xattn_ln2_b': (0.0, 0.419),
     'L0_xattn_ln3_g': (1.0, 0.2),
     'L0_xattn_ln3_b': (0.0, 0.1),
     'L1_xattn_qn_w': (1.0, 0.573),
     'L1_xattn_qn_b': (0.0, 0.551),
     'L1_xattn_cn_w': (1.0, 0.2),
     'L1_xattn_cn_b': (0.0, 0.1),
     'L1_xattn_n2_w': (1.0, 0.2),
     'L1_xattn_n2_b': (0.0, 0.1),
     'L1_xattn_proj_b': (0.0, 0.1),
     'L1_xattn_fc1_b': (0.0, 0.1),
     'L1_xattn_fc2_b': (0.0, 0.1)}
    factors = {}
    for name, (base, spread) in spreads.items():
        noise = np.random.default_rng([zlib.crc32(name.encode()), seed]).standard_normal(out[name].shape)
        drawn = base * np.exp(spread * noise) if base else spread * noise
        out[name] = jnp.asarray(drawn.astype(out[name].dtype))
    for name, factor in factors.items():
        out[name] = (out[name] * factor).astype(out[name].dtype)
    return out
```

```python
import concourse.bass as bass
from concourse import mybir
from contextlib import ExitStack

F32 = mybir.dt.float32
F32R = mybir.dt.float32r
U8 = mybir.dt.uint8
ACT = mybir.ActivationFunctionType
ALU = mybir.AluOpType
AX = mybir.AxisListType

P = 128
BATCH = 64
SEQ = 256
CTX = 120
D = 256
FF = 1024
HEADS = 16
DK = D // HEADS
KT = D // P
QT = SEQ // P
PAIRS = HEADS // 2
GROUPS = 4
SLOTS = 2
ITERATIONS = BATCH // SLOTS
EPS = 1e-5
MASKED = -(2.0 ** 100)
RING = 6
FRING = 4
PRING = 3


def head_place(h):
    t, g = divmod(h, 8)
    return (g // 2) * 2 + t, g % 2


class Signal:

    def __init__(self, sem, step=1):
        self.sem, self.step, self.events = sem, step, {}

    def event(self, key):
        assert key not in self.events, key
        self.events[key] = len(self.events)

    def start(self, engine):
        if self.events:
            engine.sem_inc(self.sem, self.step * len(self.events))

    def value(self, turn, key, back=0):
        n = len(self.events)
        return turn * (n * self.step) + (n * (1 - back) + self.events[key] + 1) * self.step


def ring_before(n, total, size):
    if n >= size:
        return n - size, 0
    last = total - 1 - (total - 1 - n) % size
    return last, 1


def layer(nc, which, x_in, ctx_in, mask_in, x_out, weights, vectors):
    first = which == 0
    attentions = ["sa", "ca"] if first else ["ca"]
    masked = not first

    stack = ExitStack()
    with stack:
        def sb(name, shape, dt):
            return stack.enter_context(nc.sbuf_tensor(f"L{which}_{name}", shape, dt))

        def signal(name, step=1):
            s = Signal(stack.enter_context(nc.semaphore(f"L{which}_{name}")), step)
            signals[name] = s
            return s

        signals = {}

        square = {"sa": ("sa_q", "sa_k", "sa_v", "sa_o"), "ca": ("ca_q", "ca_k", "ca_v", "ca_o")}
        names = [n for a in attentions for n in square[a]]
        w_hi = {n: sb(f"{n}_hi", [P, KT, D], F32R) for n in names}
        w_lo = {n: sb(f"{n}_lo", [P, KT, D], F32R) for n in names}
        w1_hi, w1_lo = sb("w1_hi", [P, KT, FF], F32R), sb("w1_lo", [P, KT, FF], F32R)
        w2_hi, w2_lo = sb("w2_hi", [P, FF // P, D], F32R), sb("w2_lo", [P, FF // P, D], F32R)
        ln_names = (["ln1", "ln2", "ln3"] if first else ["cn", "qn", "n2"])
        gain = {n: sb(f"{n}_gain", [P, KT], F32) for n in ln_names}
        shift = {n: sb(f"{n}_shift", [P, KT], F32) for n in ln_names}
        b1 = sb("b1", [P, FF // P], F32)
        b2 = sb("b2", [P, D], F32)
        proj_b = None if first else sb("proj_b", [P, D], F32)
        ident = sb("ident", [P, P], F32)
        ident_r = sb("ident_r", [P, P], F32R)
        causal = sb("causal", [P, P], F32R) if first else None
        minus_half = sb("minus_half", [P, QT], F32)
        ones_row = sb("ones_row", [1, HEADS * SEQ // 4], F32)

        split = sb("split", [P, FRING, 512], F32)
        probs = sb("probs", [P, PRING, 4 * 384], F32)
        heads_out = sb("heads_out", [P, GROUPS, SEQ], F32)
        slot = []
        for s in range(SLOTS):
            slot.append(dict(
                xin=sb(f"xin{s}", [P, QT, D], F32), x=sb(f"x{s}", [P, QT, D], F32),
                z=sb(f"z{s}", [P, QT, D], F32), cin=sb(f"cin{s}", [CTX, D], F32),
                cz=None if first else sb(f"cz{s}", [CTX, D], F32),
                ht_hi=sb(f"ht_hi{s}", [P, KT, SEQ], F32R), ht_lo=sb(f"ht_lo{s}", [P, KT, SEQ], F32R),
                ct_hi=sb(f"ct_hi{s}", [P, KT, CTX], F32R), ct_lo=sb(f"ct_lo{s}", [P, KT, CTX], F32R),
                big_hi=sb(f"big_hi{s}", [P, 4, SEQ], F32R), big_lo=sb(f"big_lo{s}", [P, 4, SEQ], F32R),
                v=sb(f"v{s}", [P, 2 if first else 1, HEADS, 32], F32),
                qs=sb(f"qs{s}", [P, PAIRS, SEQ], F32R),
                ks=sb(f"ks{s}", [P, PAIRS, 2, SEQ if first else CTX], F32R),
                neg=sb(f"neg{s}", [P, QT, P], F32), c=sb(f"c{s}", [HEADS, SEQ], F32R),
                stats=sb(f"stats{s}", [P, QT, 6], F32), mv=sb(f"mv{s}", [P, QT, 2], F32),
                rstd=sb(f"rstd{s}", [P, QT], F32), rden=sb(f"rden{s}", [P, QT, HEADS], F32),
                mask8=None if first else sb(f"mask8{s}", [P, QT, CTX], U8),
                mask=None if first else sb(f"mask{s}", [P, QT, CTX], F32R)))

        ring = stack.enter_context(nc.psum_tensor(f"L{which}_ring", [P, RING, 512], F32))
        acc = stack.enter_context(nc.psum_tensor(f"L{which}_acc", [P, 2, 512], F32))

        ring_ready = signal("ring_ready")
        ring_freed_act = signal("ring_freed_act")
        ring_freed_dve = signal("ring_freed_dve")
        f_ready = signal("f_ready")
        hi_ready = signal("hi_ready")
        lo_ready = signal("lo_ready")
        v_ready = signal("v_ready")
        neg_ready = signal("neg_ready")
        c_ready = signal("c_ready")
        exp_ready = signal("exp_ready")
        probs_used = signal("probs_used")
        acc_ready = [signal(f"acc_ready{b}") for b in range(2)]
        acc_freed = [signal(f"acc_freed{b}") for b in range(2)]
        heads_ready = signal("heads_ready")
        rden_ready = signal("rden_ready")
        oq_ready = signal("oq_ready")
        x_ready = signal("x_ready")
        stats_ready = signal("stats_ready")
        mv_ready = signal("mv_ready")
        eps_ready = signal("eps_ready")
        rstd_ready = signal("rstd_ready")
        z_ready = signal("z_ready")
        bias_ready = signal("bias_ready")
        mask_ready = signal("mask_ready")
        xin_loaded = [signal(f"xin_loaded{s}", 16) for s in range(SLOTS)]
        cin_loaded = [signal(f"cin_loaded{s}", 16) for s in range(SLOTS)]
        mask_loaded = [signal(f"mask_loaded{s}", 16) for s in range(SLOTS)]
        qk_loaded = [signal(f"qk_loaded{s}", 16) for s in range(SLOTS)]
        c_loaded = [signal(f"c_loaded{s}", 16) for s in range(SLOTS)]
        stored = [signal(f"stored{s}", 16) for s in range(SLOTS)]
        stats_seen = stack.enter_context(nc.semaphore(f"L{which}_stats_seen"))
        w_loaded = stack.enter_context(nc.semaphore(f"L{which}_w_loaded"))
        w_split = stack.enter_context(nc.semaphore(f"L{which}_w_split"))
        w_lead = stack.enter_context(nc.semaphore(f"L{which}_w_lead"))
        vec_loaded = stack.enter_context(nc.semaphore(f"L{which}_vec_loaded"))
        cleared = stack.enter_context(nc.semaphore(f"L{which}_cleared"))
        built = stack.enter_context(nc.semaphore(f"L{which}_built"))
        ones_set = stack.enter_context(nc.semaphore(f"L{which}_ones_set"))
        pads_set = stack.enter_context(nc.semaphore(f"L{which}_pads_set"))

        order = []

        def both(*stages):
            for stage in stages:
                for s in range(SLOTS):
                    order.append((s, *stage))

        def attention(a, ln):
            both(("stats", ln), ("normal", ln), ("q", a), ("k", a), ("v", a), ("max", a), ("c", a))
            for s in range(SLOTS):
                order.append((s, "attend", a))
                order.append((s, "turned", a))
            both(("o_split", a), ("o_proj", a))

        if first:
            both(("context",))
            attention("sa", "ln1")
            attention("ca", "ln2")
            ffn_ln = "ln3"
        else:
            both(("stats", "cn"), ("normal", "cn"))
            attention("ca", "qn")
            ffn_ln = "n2"
        both(("stats", ffn_ln), ("normal", ffn_ln), ("up", 0), ("up", 1), ("down", 0), ("up", 2), ("down", 1),
             ("up", 3), ("down", 2), ("down", 3))

        ring_jobs, ring_reader, f_jobs, groups = [], [], [], []

        def ring_job(key, reader):
            ring_jobs.append(key)
            ring_reader.append(reader)
            ring_ready.event(key)
            (ring_freed_act if reader == "act" else ring_freed_dve).event(key)

        def f_job(key):
            ring_job(key, "act")
            f_jobs.append(key)
            for sig in (f_ready, hi_ready, lo_ready):
                sig.event(key)

        def score_jobs(a):
            return 3 if a == "sa" else 2

        def max_jobs(a):
            return 12 if a == "sa" else 8

        for s, stage, *arg in order:
            key = (s, stage, *arg)
            if stage == "context":
                f_job(key)
            elif stage == "stats":
                for sig in (stats_ready, mv_ready, eps_ready, rstd_ready):
                    sig.event(key)
            elif stage == "normal":
                z_ready.event(key)
                f_job(key)
            elif stage in ("q", "k"):
                f_job(key)
            elif stage == "v":
                ring_job(key, "act")
                v_ready.event(key)
            elif stage == "max":
                for n in range(max_jobs(arg[0])):
                    ring_job((*key, n), "dve")
                neg_ready.event(key)
            elif stage == "c":
                ring_job(key, "dve")
                c_ready.event(key)
            elif stage == "attend":
                for g in range(GROUPS):
                    for n in range(score_jobs(arg[0])):
                        ring_job((*key, g, n), "act")
                        exp_ready.event((*key, g, n))
                    groups.append((*key, g))
                    probs_used.event((*key, g))
                for b in range(2):
                    acc_ready[b].event(key)
                    acc_freed[b].event(key)
                    heads_ready.event((*key, b))
            elif stage == "turned":
                for u in range(QT):
                    ring_job((*key, u), "dve")
                    rden_ready.event((*key, u))
                oq_ready.event(key)
            elif stage == "o_split":
                f_job(key)
            elif stage == "o_proj":
                ring_job(key, "dve")
                x_ready.event(key)
            elif stage == "up":
                f_job(key)
            elif stage == "down" and arg[0] == 3:
                acc_ready[s].event((s, "down"))
                acc_freed[s].event((s, "down"))
                x_ready.event((s, "down"))
        biased = [(s, "normal", ln) for s, stage, ln in [(*o, None)[:3] for o in order]
                  if stage == "normal" and ln in (ffn_ln, "qn")]
        for key in biased:
            bias_ready.event(key)
        if masked:
            for s in range(SLOTS):
                mask_ready.event(s)
        for s in range(SLOTS):
            xin_loaded[s].event("x")
            cin_loaded[s].event("c")
            if masked:
                mask_loaded[s].event("m")
            stored[s].event("x")
            for a in attentions:
                for n in range(14):
                    qk_loaded[s].event((a, n))
                for n in range(2):
                    c_loaded[s].event((a, n))

        def bank_of(key):
            return ring[:, ring_jobs.index(key) % RING, :]

        def tile_of(key):
            return split[:, f_jobs.index(key) % FRING, :]

        def probs_of(key):
            return probs[:, groups.index(key) % PRING, :]

        def split_to(key):
            s, stage, *arg = key
            v = slot[s]
            if stage == "context" or arg[0] == "cn":
                return v["ct_hi"][:, :, :].rearrange("p k n -> p (k n)"), \
                    v["ct_lo"][:, :, :].rearrange("p k n -> p (k n)"), KT * CTX
            if stage == "normal":
                return v["ht_hi"][:, :, :].rearrange("p k n -> p (k n)"), \
                    v["ht_lo"][:, :, :].rearrange("p k n -> p (k n)"), KT * SEQ
            half = {"q": 0, "k": 1, "o_split": 0}[stage] if stage != "up" else arg[0] % 2
            width = 2 * (CTX if stage == "k" and arg[0] == "ca" else SEQ)
            hi = v["big_hi"][:, :, :].rearrange("p k n -> p (k n)")[:, 512 * half:512 * half + width]
            lo = v["big_lo"][:, :, :].rearrange("p k n -> p (k n)")[:, 512 * half:512 * half + width]
            return hi, lo, width

        def keys_of(a):
            return SEQ if a == "sa" else CTX

        loads = []
        for n in names:
            loads.append((n, weights[n].rearrange("(k p) n -> p k n", p=P), KT, D, w_hi[n], w_lo[n]))
        loads.append(("w1", weights["w1"].rearrange("(k p) n -> p k n", p=P), KT, FF, w1_hi, w1_lo))
        loads.append(("w2", weights["w2"].rearrange("(k p) n -> p k n", p=P), FF // P, D, w2_hi, w2_lo))
        vector_loads = [(gain[n], vectors[n + "_g"]) for n in ln_names] + \
            [(shift[n], vectors[n + "_b"]) for n in ln_names] + [(b1, vectors["b1"])]
        row_loads = [(b2, vectors["b2"])] + ([] if first else [(proj_b, vectors["proj_b"])])
        all_loads = 16 * (len(vector_loads) + len(row_loads))

        block = stack.enter_context(nc.Block())

        @block.sync
        def _(sp):
            with nc.allow_non_contiguous_dma(reason="one value per partition, once"):
                for dst, src in vector_loads:
                    sp.dma_start(dst[:, :], src.rearrange("(k p) -> p k", p=P)).then_inc(vec_loaded, 16)
            for dst, src in row_loads:
                sp.dma_start(dst[:, :], src.rearrange("(a n) -> a n", a=1).to_broadcast([P, D]))\
                    .then_inc(vec_loaded, 16)
            for n, (_, src, kt, width, _, _) in enumerate(loads):
                if n:
                    sp.wait_ge(w_split, n)
                stage = split[:, :, :].rearrange("p r n -> p (r n)")[:, 0:kt * width]
                sp.dma_start(stage.rearrange("p (k n) -> p k n", k=kt), src).then_inc(w_loaded, 16)
            sp.wait_ge(cleared, 1)
            sp.wait_ge(ones_set, 1)
            for s in range(SLOTS):
                keys = SEQ if first else CTX
                for e in range(2):
                    dst = slot[s]["ks"][64 * e + 48:64 * e + 49, :, e, :].bitcast(F32)
                    sp.dma_start(dst, ones_row[0:1, 0:PAIRS * keys // 2].rearrange("a (k n) -> a k n", n=keys)
                                 if False else ones_row[0:1, 0:keys].rearrange("a (k n) -> a k n", k=1)
                                 .to_broadcast([1, PAIRS, keys])).then_inc(pads_set, 16)
            for s in range(SLOTS):
                for sig in (xin_loaded[s], cin_loaded[s], mask_loaded[s], qk_loaded[s], c_loaded[s], stored[s]):
                    sig.start(sp)

            def scatter(turn, s, a, what):
                v = slot[s]
                sp.wait_ge(lo_ready.sem, lo_ready.value(turn, (s, what, a)))
                n = keys_of(a) if what == "k" else SEQ
                off = 512 if what == "k" else 0
                hi = v["big_hi"][:, :, :].rearrange("p k n -> p (k n)").bitcast(F32)
                lo = v["big_lo"][:, :, :].rearrange("p k n -> p (k n)").bitcast(F32)
                parts = (hi, lo, hi) if what == "q" else (hi, hi, lo)
                for e in range(2):
                    for c, part in enumerate(parts):
                        rows = slice(64 * e + 16 * c, 64 * e + 16 * c + 16)
                        if what == "q":
                            dst = v["qs"][rows, :, :].bitcast(F32)
                        else:
                            dst = v["ks"][rows, :, e, 0:n].bitcast(F32)
                        src = part[e::2, off:off + 2 * n]
                        if what == "k":
                            src = src.rearrange("p (k n) -> p k n", k=2)
                        sp.dma_start(dst, src).then_inc(qk_loaded[s].sem, 16)

            with sp.Fori(0, ITERATIONS) as turn:
                for s in range(SLOTS):
                    v = slot[s]
                    sp.wait_ge(x_ready.sem, x_ready.value(turn, (s, "o_proj", attentions[0]), 1))
                    seq = turn * SLOTS + s
                    sp.dma_start(v["xin"][:, :, :], x_in[bass.ds(seq * SEQ, SEQ), :]
                                 .rearrange("(u p) d -> p u d", p=P)).then_inc(xin_loaded[s].sem, 16)
                    sp.dma_start(v["cin"][:, :], ctx_in[bass.ds(seq * CTX, CTX), :])\
                        .then_inc(cin_loaded[s].sem, 16)
                    if masked:
                        sp.dma_start(v["mask8"][:, :, :], mask_in[bass.ds(seq * SEQ, SEQ), :]
                                     .rearrange("(u p) d -> p u d", p=P)).then_inc(mask_loaded[s].sem, 16)
                for s, stage, *arg in order:
                    v = slot[s]
                    if stage == "q":
                        scatter(turn, s, arg[0], "q")
                        for e in range(2):
                            row = 64 * e + 48
                            sp.dma_start(v["qs"][row:row + 1, :, :].bitcast(F32),
                                         v["qs"][row + 1:row + 2, :, :].bitcast(F32))\
                                .then_inc(qk_loaded[s].sem, 16)
                    elif stage == "k":
                        scatter(turn, s, arg[0], "k")
                    elif stage == "c":
                        sp.wait_ge(c_ready.sem, c_ready.value(turn, (s, "c", arg[0])))
                        for e in range(2):
                            row = 64 * e + 48
                            sp.dma_start(v["qs"][row:row + 1, :, :].bitcast(F32),
                                         v["c"][PAIRS * e:PAIRS * e + PAIRS, :].bitcast(F32))\
                                .then_inc(c_loaded[s].sem, 16)
                for s in range(SLOTS):
                    sp.wait_ge(x_ready.sem, x_ready.value(turn, (s, "down")))
                    sp.dma_start(x_out[bass.ds((turn * SLOTS + s) * SEQ, SEQ), :]
                                 .rearrange("(u p) d -> p u d", p=P), slot[s]["x"][:, :, :])\
                        .then_inc(stored[s].sem, 16)
            for s in range(SLOTS):
                sp.wait_ge(stored[s].sem, 16 * (ITERATIONS + 1))

        @block.gpsimd
        def _(pool):
            pool.memset(ident[:, :], 0.0).then_inc(built, 1)
            pool.memset(minus_half[:, :], -0.5)
            pool.memset(ones_row[:, :], 1.0).then_inc(ones_set, 1)
            pool.wait_ge(built, 1)
            pool.affine_select(out=ident[:, :], in_=ident[:, :], compare_op=ALU.not_equal, fill=1.0,
                               base=0, pattern=[[-1, P]], channel_multiplier=1).then_inc(built, 1)
            for sig in (lo_ready, rstd_ready, bias_ready):
                sig.start(pool)
            pool.wait_ge(vec_loaded, all_loads)
            with pool.Fori(0, ITERATIONS) as turn:
                for s, stage, *arg in order:
                    v = slot[s]
                    key = (s, stage, *arg)
                    if stage == "stats":
                        rows = CTX if arg[0] == "cn" else P
                        us = 1 if arg[0] == "cn" else QT
                        pool.wait_ge(eps_ready.sem, eps_ready.value(turn, key))
                        pool.tensor_tensor(v["rstd"][0:rows, 0:us], v["rstd"][0:rows, 0:us],
                                           minus_half[0:rows, 0:us], ALU.pow).then_inc(rstd_ready.sem, 1)
                        continue
                    if key in lo_ready.events:
                        hi, lo, width = split_to(key)
                        pool.wait_ge(hi_ready.sem, hi_ready.value(turn, key))
                        pool.tensor_tensor(lo, tile_of(key)[:, 0:width], hi.bitcast(F32), ALU.subtract)\
                            .then_inc(lo_ready.sem, 1)
                    if key in bias_ready.events:
                        src, row = (v["x"], b2) if arg[0] == ffn_ln else (v["xin"], proj_b)
                        pool.wait_ge(z_ready.sem, z_ready.value(turn, key))
                        pool.tensor_tensor(src[:, :, :], src[:, :, :],
                                           row[:, :].rearrange("p (a n) -> p a n", a=1).to_broadcast([P, QT, D]),
                                           ALU.add).then_inc(bias_ready.sem, 1)

        @block.scalar
        def _(act):
            for sig in (ring_freed_act, f_ready, v_ready, exp_ready, acc_freed[0], acc_freed[1], heads_ready):
                sig.start(act)
            act.wait_ge(vec_loaded, all_loads)
            act.wait_ge(w_split, len(loads))
            act.wait_ge(cleared, 1)

            def f_tile(turn, key):
                act.wait_ge(ring_ready.sem, ring_ready.value(turn, key))
                before, back = ring_before(f_jobs.index(key), len(f_jobs), FRING)
                act.wait_ge(lo_ready.sem, lo_ready.value(turn, f_jobs[before], back))

            with act.Fori(0, ITERATIONS) as turn:
                for s, stage, *arg in order:
                    v = slot[s]
                    key = (s, stage, *arg)
                    if stage in ("context", "q", "k", "o_split"):
                        width = split_to(key)[2]
                        f_tile(turn, key)
                        act.activation(tile_of(key)[:, 0:width], bank_of(key)[:, 0:width], ACT.Copy,
                                       scale=DK ** -0.5 if stage == "k" else 1.0).then_inc(f_ready.sem, 1)
                        act.wait_ge(f_ready.sem, f_ready.value(turn, key))
                        act.sem_inc(ring_freed_act.sem, 1)
                    elif stage == "normal":
                        width = split_to(key)[2] // KT
                        f_tile(turn, key)
                        for k in range(KT):
                            last = act.activation(tile_of(key)[:, k * width:(k + 1) * width],
                                                  bank_of(key)[:, k * width:(k + 1) * width], ACT.Identity,
                                                  bias=shift[arg[0]][:, k:k + 1], scale=gain[arg[0]][:, k:k + 1])
                        last.then_inc(f_ready.sem, 1)
                        act.wait_ge(f_ready.sem, f_ready.value(turn, key))
                        act.sem_inc(ring_freed_act.sem, 1)
                    elif stage == "v":
                        act.wait_ge(ring_ready.sem, ring_ready.value(turn, key))
                        rows, tiles = (P, 2) if arg[0] == "sa" else (CTX, 1)
                        for k in range(tiles):
                            last = act.activation(
                                v["v"][0:rows, k, :, 0:DK],
                                bank_of(key)[0:rows, k * D:(k + 1) * D].rearrange("p (h d) -> p h d", d=DK),
                                ACT.Copy)
                        last.then_inc(v_ready.sem, 1)
                        act.wait_ge(v_ready.sem, v_ready.value(turn, key))
                        act.sem_inc(ring_freed_act.sem, 1)
                    elif stage == "attend":
                        rows = P if arg[0] == "sa" else CTX
                        for g in range(GROUPS):
                            before, back = ring_before(groups.index((*key, g)), len(groups), PRING)
                            act.wait_ge(probs_used.sem, probs_used.value(turn, groups[before], back))
                            for n in range(score_jobs(arg[0])):
                                job = (*key, g, n)
                                act.wait_ge(ring_ready.sem, ring_ready.value(turn, job))
                                act.activation(probs_of((*key, g))[0:rows, 512 * n:512 * n + 512],
                                               bank_of(job)[0:rows, :], ACT.Exp).then_inc(exp_ready.sem, 1)
                                act.wait_ge(exp_ready.sem, exp_ready.value(turn, job))
                                act.sem_inc(ring_freed_act.sem, 1)
                        for b in range(2):
                            act.wait_ge(acc_ready[b].sem, acc_ready[b].value(turn, key))
                            act.activation(heads_out[:, 2 * b:2 * b + 2, :].rearrange("p g n -> p (g n)"),
                                           acc[:, b, :], ACT.Copy).then_inc(heads_ready.sem, 1)
                            act.wait_ge(heads_ready.sem, heads_ready.value(turn, (*key, b)))
                            act.sem_inc(acc_freed[b].sem, 1)
                    elif stage == "up":
                        f_tile(turn, key)
                        for m in range(2):
                            last = act.activation(tile_of(key)[:, m * SEQ:(m + 1) * SEQ],
                                                  bank_of(key)[:, m * SEQ:(m + 1) * SEQ],
                                                  ACT.Relu if first else ACT.Gelu,
                                                  bias=b1[:, 2 * arg[0] + m:2 * arg[0] + m + 1])
                        last.then_inc(f_ready.sem, 1)
                        act.wait_ge(f_ready.sem, f_ready.value(turn, key))
                        act.sem_inc(ring_freed_act.sem, 1)

        @block.vector
        def _(dve):
            for s in range(SLOTS):
                v = slot[s]
                dve.memset(v["qs"][:, :, :].bitcast(F32), 0.0)
                dve.memset(v["ks"][:, :, :, :].bitcast(F32), 0.0)
                dve.memset(v["v"][:, :, :, DK:32], 0.0)
                last = dve.memset(v["neg"][:, :, :], 0.0)
            last.then_inc(w_lead, 1)
            dve.wait_ge(w_lead, 1)
            for s in range(SLOTS):
                last = dve.memset(slot[s]["v"][:, :, :, DK:DK + 1], 1.0)
            last.then_inc(cleared, 1)
            for n, (name, _, kt, width, hi, lo) in enumerate(loads):
                dve.wait_ge(w_loaded, 16 * (n + 1))
                stage = split[:, :, :].rearrange("p r n -> p (r n)")[:, 0:kt * width]
                if name[-2:] in ("_q", "_k"):
                    srcs = [stage.rearrange("p (k g d) -> p k d g", k=kt * KT, d=DK)]
                    his = [hi[:, :, :].rearrange("p k (t d g) -> p (k t) d g", t=KT, d=DK)]
                    los = [lo[:, :, :].rearrange("p k (t d g) -> p (k t) d g", t=KT, d=DK)]
                else:
                    srcs = [stage]
                    his = [hi[:, :, :].rearrange("p k n -> p (k n)")]
                    los = [lo[:, :, :].rearrange("p k n -> p (k n)")]
                dve.tensor_copy(his[0], srcs[0]).then_inc(w_lead, 1)
                dve.wait_ge(w_lead, n + 2)
                dve.tensor_tensor(los[0], srcs[0], his[0].bitcast(F32), ALU.subtract).then_inc(w_split, 1)
            dve.wait_ge(built, 2)
            if first:
                dve.tensor_copy(ident_r[:, :], ident[:, :])
                dve.tensor_tensor_scan(slot[0]["z"][:, 0, 0:P], ident[:, :], ident[:, :], 0.0, ALU.max, ALU.max)\
                    .then_inc(built, 1)
                dve.wait_ge(built, 3)
                dve.tensor_tensor(slot[0]["z"][:, 0, 0:P], slot[0]["z"][:, 0, 0:P], ident[:, :], ALU.subtract)\
                    .then_inc(built, 1)
                dve.wait_ge(built, 4)
                dve.tensor_scalar(causal[:, :], slot[0]["z"][:, 0, 0:P], MASKED, None, ALU.mult)\
                    .then_inc(built, 1)
            else:
                dve.tensor_copy(ident_r[:, :], ident[:, :]).then_inc(built, 3)
            for sig in (ring_freed_dve, hi_ready, neg_ready, c_ready, rden_ready, oq_ready, x_ready,
                        stats_ready, mv_ready, eps_ready, z_ready, mask_ready):
                sig.start(dve)

            with dve.Fori(0, ITERATIONS) as turn:
                for s, stage, *arg in order:
                    v = slot[s]
                    key = (s, stage, *arg)
                    ctx_norm = bool(arg) and arg[0] == "cn"
                    rows, us = (CTX, 1) if ctx_norm else (P, QT)
                    if stage in ("stats", "normal"):
                        at_start = arg[0] in ("ln1", "qn")
                        src = v["cin"][:, :].rearrange("p (u d) -> p u d", u=1) if ctx_norm else \
                            v["xin"] if at_start else v["x"]
                    if stage == "stats":
                        if ctx_norm:
                            dve.wait_ge(cin_loaded[s].sem, cin_loaded[s].value(turn, "c"))
                        elif at_start:
                            dve.wait_ge(xin_loaded[s].sem, xin_loaded[s].value(turn, "x"))
                        else:
                            a_before = "sa" if arg[0] == "ln2" else "ca"
                            dve.wait_ge(x_ready.sem, x_ready.value(turn, (s, "o_proj", a_before)))
                        for u in range(us):
                            last = dve.bn_stats(v["stats"][0:rows, u, :], src[:, u, :])
                        last.then_inc(stats_ready.sem, 1)
                        dve.wait_ge(stats_ready.sem, stats_ready.value(turn, key))
                        dve.sem_inc(stats_seen, 1)
                        for u in range(us):
                            last = dve.bn_aggr(v["mv"][0:rows, u, :], v["stats"][0:rows, u, :])
                        last.then_inc(mv_ready.sem, 1)
                        dve.wait_ge(mv_ready.sem, mv_ready.value(turn, key))
                        dve.tensor_scalar(v["rstd"][0:rows, 0:us], v["mv"][0:rows, 0:us, 1], EPS, None,
                                          ALU.add).then_inc(eps_ready.sem, 1)
                        if masked and ctx_norm:
                            dve.wait_ge(mask_loaded[s].sem, mask_loaded[s].value(turn, "m"))
                            dve.tensor_scalar(v["mask"][:, :, :], v["mask8"][:, :, :], MASKED, None, ALU.mult)\
                                .then_inc(mask_ready.sem, 1)
                    if stage == "normal":
                        dst = v["cz"][:, :].rearrange("p (u d) -> p u d", u=1) if ctx_norm else v["z"]
                        dve.wait_ge(rstd_ready.sem, rstd_ready.value(turn, (s, "stats", arg[0])))
                        for u in range(us):
                            last = dve.tensor_scalar(dst[:, u, :], src[:, u, :], v["mv"][0:rows, u, 0:1],
                                                     v["rstd"][0:rows, u:u + 1], ALU.subtract, ALU.mult)
                        last.then_inc(z_ready.sem, 1)
                    if key in hi_ready.events:
                        hi, _, width = split_to(key)
                        dve.wait_ge(f_ready.sem, f_ready.value(turn, key))
                        dve.tensor_copy(hi, tile_of(key)[:, 0:width]).then_inc(hi_ready.sem, 1)
                    elif stage == "max":
                        for n in range(max_jobs(arg[0])):
                            job = (*key, n)
                            dve.wait_ge(ring_ready.sem, ring_ready.value(turn, job))
                            neg = v["neg"][:, :, 0:HEADS].rearrange("p u (e r) -> p u r e", e=2)
                            if arg[0] == "ca":
                                out = neg[:, :, n, :]
                                scores = bank_of(job)[:, 0:QT * 2 * CTX].rearrange("p (u e k) -> p u e k", u=QT, e=2)
                            elif n < PAIRS:
                                out = neg[:, 1, n, :]
                                scores = bank_of(job).rearrange("p (e k) -> p e k", e=2)
                            else:
                                out = neg[:, 0, 2 * (n - PAIRS):2 * (n - PAIRS) + 2, :]
                                scores = bank_of(job).rearrange("p (r e k) -> p r e k", r=2, e=2)
                            last = dve.tensor_reduce(out, scores, AX.X, ALU.max, negate=True)
                            last.then_inc(ring_freed_dve.sem, 1)
                        dve.wait_ge(ring_freed_dve.sem, ring_freed_dve.value(turn, job))
                        dve.sem_inc(neg_ready.sem, 1)
                    elif stage == "c":
                        dve.wait_ge(ring_ready.sem, ring_ready.value(turn, key))
                        dve.tensor_copy(v["c"][:, :], bank_of(key)[0:HEADS, 0:SEQ]).then_inc(c_ready.sem, 1)
                        dve.wait_ge(c_ready.sem, c_ready.value(turn, key))
                        dve.sem_inc(ring_freed_dve.sem, 1)
                    elif stage == "turned":
                        for u in range(QT):
                            job = (*key, u)
                            dve.wait_ge(ring_ready.sem, ring_ready.value(turn, job))
                            o = bank_of(job).rearrange("p (h c) -> p h c", c=32)
                            dve.reciprocal(v["rden"][:, u, :], o[:, :, DK]).then_inc(rden_ready.sem, 1)
                            dve.wait_ge(rden_ready.sem, rden_ready.value(turn, job))
                            dve.tensor_tensor(
                                v["z"][:, u, :].rearrange("p (h d) -> p h d", d=DK), o[:, :, 0:DK],
                                v["rden"][:, u, :].rearrange("p (h d) -> p h d", d=1).to_broadcast([P, HEADS, DK]),
                                ALU.mult).then_inc(ring_freed_dve.sem, 1)
                        dve.wait_ge(ring_freed_dve.sem, ring_freed_dve.value(turn, job))
                        dve.sem_inc(oq_ready.sem, 1)
                    elif stage == "o_proj":
                        src = v["xin"] if arg[0] == attentions[0] else v["x"]
                        if arg[0] == attentions[0]:
                            dve.wait_ge(stored[s].sem, stored[s].value(turn, "x", 1))
                        if not first:
                            dve.wait_ge(bias_ready.sem, bias_ready.value(turn, (s, "normal", "qn")))
                        dve.wait_ge(ring_ready.sem, ring_ready.value(turn, key))
                        dve.tensor_tensor(v["x"][:, :, :].rearrange("p u d -> p (u d)"), bank_of(key),
                                          src[:, :, :].rearrange("p u d -> p (u d)"), ALU.add)\
                            .then_inc(x_ready.sem, 1)
                        dve.wait_ge(x_ready.sem, x_ready.value(turn, key))
                        dve.sem_inc(ring_freed_dve.sem, 1)
                    elif stage == "down" and arg[0] == 3:
                        dve.wait_ge(bias_ready.sem, bias_ready.value(turn, (s, "normal", ffn_ln)))
                        dve.wait_ge(acc_ready[s].sem, acc_ready[s].value(turn, (s, "down")))
                        dve.tensor_tensor(v["x"][:, :, :].rearrange("p u d -> p (u d)"), acc[:, s, :],
                                          v["x"][:, :, :].rearrange("p u d -> p (u d)"), ALU.add)\
                            .then_inc(x_ready.sem, 1)
                        dve.wait_ge(x_ready.sem, x_ready.value(turn, (s, "down")))
                        dve.sem_inc(acc_freed[s].sem, 1)

        @block.tensor
        def _(pe):
            for sig in (ring_ready, probs_used, acc_ready[0], acc_ready[1]):
                sig.start(pe)
            pe.wait_ge(w_split, len(loads))
            pe.wait_ge(built, 5)
            pe.wait_ge(pads_set, 16 * 2 * SLOTS)

            def take_bank(turn, key):
                n = ring_jobs.index(key)
                before, back = ring_before(n, len(ring_jobs), RING)
                freed = ring_freed_act if ring_reader[before] == "act" else ring_freed_dve
                pe.wait_ge(freed.sem, freed.value(turn, ring_jobs[before], back))
                return ring[:, n % RING, :]

            def product(out, stationary, moving, start=True, stop=True):
                terms = [(a, b) for a, b in ((0, 0), (1, 0), (0, 1))]
                tiles = len(stationary[0])
                for k in range(tiles):
                    for i, (a, b) in enumerate(terms):
                        last = pe.matmul(out, stationary[a][k], moving[b][k], start=start and k == 0 and i == 0,
                                         stop=stop and k == tiles - 1 and i == 2)
                return last

            def split_ready(turn, key):
                pe.wait_ge(lo_ready.sem, lo_ready.value(turn, key))

            with pe.Fori(0, ITERATIONS) as turn:
                for s, stage, *arg in order:
                    v = slot[s]
                    key = (s, stage, *arg)
                    a = arg[0] if arg else None
                    if stage == "context" or (stage == "normal" and a == "cn"):
                        if stage == "context":
                            src = v["cin"]
                            pe.wait_ge(cin_loaded[s].sem, cin_loaded[s].value(turn, "c"))
                        else:
                            src = v["cz"]
                            pe.wait_ge(z_ready.sem, z_ready.value(turn, key))
                        bank = take_bank(turn, key)
                        for k in range(KT):
                            last = pe.transpose(bank[:, k * CTX:(k + 1) * CTX], src[:, k * P:(k + 1) * P],
                                                ident[0:CTX, 0:CTX])
                        last.then_inc(ring_ready.sem, 1)
                    elif stage in ("normal", "o_split"):
                        if stage == "normal":
                            pe.wait_ge(z_ready.sem, z_ready.value(turn, key))
                        else:
                            pe.wait_ge(oq_ready.sem, oq_ready.value(turn, (s, "turned", a)))
                        bank = take_bank(turn, key)
                        for k in range(KT):
                            for u in range(QT):
                                last = pe.transpose(bank[:, (k * QT + u) * P:(k * QT + u + 1) * P],
                                                    v["z"][:, u, k * P:(k + 1) * P], ident[:, :])
                        last.then_inc(ring_ready.sem, 1)
                    elif stage in ("q", "k"):
                        if stage == "q":
                            ln = {"sa": "ln1", "ca": "ln2" if first else "qn"}[a]
                            split_ready(turn, (s, "normal", ln))
                        elif a == "ca":
                            split_ready(turn, (s, "context") if first else (s, "normal", "cn"))
                        n = SEQ if stage == "q" or a == "sa" else CTX
                        act_hi, act_lo = (v["ht_hi"], v["ht_lo"]) if n == SEQ else (v["ct_hi"], v["ct_lo"])
                        w = f"{a}_{stage}"
                        bank = take_bank(turn, key)
                        for t in range(KT):
                            last = product(bank[:, t * n:(t + 1) * n],
                                           [[x[:, k, t * P:(t + 1) * P] for k in range(KT)] for x in (w_hi[w], w_lo[w])],
                                           [[x[:, k, :] for k in range(KT)] for x in (act_hi, act_lo)])
                        last.then_inc(ring_ready.sem, 1)
                    elif stage == "v":
                        act_hi, act_lo, tiles, rows = (v["ht_hi"], v["ht_lo"], 2, P) if a == "sa" else \
                            (v["ct_hi"], v["ct_lo"], 1, CTX)
                        w = f"{a}_v"
                        bank = take_bank(turn, key)
                        for u in range(tiles):
                            last = product(bank[0:rows, u * D:(u + 1) * D],
                                           [[x[:, k, u * P:u * P + rows] for k in range(KT)] for x in (act_hi, act_lo)],
                                           [[x[:, k, :] for k in range(KT)] for x in (w_hi[w], w_lo[w])])
                        last.then_inc(ring_ready.sem, 1)
                    elif stage == "max":
                        qs, ks = v["qs"], v["ks"]
                        pe.wait_ge(qk_loaded[s].sem, qk_loaded[s].value(turn, (a, 13)))
                        if masked:
                            pe.wait_ge(mask_ready.sem, mask_ready.value(turn, s))
                        for n in range(max_jobs(a)):
                            job = (*key, n)
                            bank = take_bank(turn, job)
                            if a == "ca":
                                for u in range(QT):
                                    half = bank[:, u * 2 * CTX:(u + 1) * 2 * CTX]
                                    last = pe.matmul(half, qs[:, n, u * P:(u + 1) * P], ks[:, n, :, 0:CTX],
                                                     start=u == 0, stop=not masked and u == 1)
                                for u in range(QT if masked else 0):
                                    half = bank[:, u * 2 * CTX:(u + 1) * 2 * CTX]
                                    last = pe.matmul(half, ident_r[:, :],
                                                     v["mask"][:, u:u + 1, :].to_broadcast([P, 2, CTX]),
                                                     start=False, stop=u == 1)
                            elif n < PAIRS:
                                pe.matmul(bank, qs[:, n, P:2 * P], ks[:, n, :, :], start=True, stop=False)
                                last = pe.matmul(bank.rearrange("p (e k) -> p e k", e=2)[:, :, P:2 * P], ident_r[:, :],
                                                 causal[:, :].rearrange("p (a k) -> p a k", a=1).to_broadcast([P, 2, P]),
                                                 start=False, stop=True)
                            else:
                                for i in range(2):
                                    pair = 2 * (n - PAIRS) + i
                                    pe.matmul(bank[:, i * 2 * P:(i + 1) * 2 * P], qs[:, pair, 0:P],
                                              ks[:, pair, :, 0:P], start=i == 0, stop=False)
                                last = pe.matmul(bank, ident_r[:, :],
                                                 causal[:, :].rearrange("p (a k) -> p a k", a=1).to_broadcast([P, 4, P]),
                                                 start=False, stop=True)
                            last.then_inc(ring_ready.sem, 1)
                    elif stage == "c":
                        pe.wait_ge(neg_ready.sem, neg_ready.value(turn, (s, "max", a)))
                        bank = take_bank(turn, key)
                        for u in range(QT):
                            last = pe.transpose(bank[:, u * P:(u + 1) * P], v["neg"][:, u, :], ident[:, :])
                        last.then_inc(ring_ready.sem, 1)
                    elif stage == "attend":
                        qs, ks = v["qs"], v["ks"]
                        keys = P if a == "sa" else CTX
                        pe.wait_ge(c_loaded[s].sem, c_loaded[s].value(turn, (a, 1)))

                        def scores(g):
                            for n in range(score_jobs(a)):
                                bank = take_bank(turn, (*key, g, n))
                                if n < 2:
                                    two = bank[0:keys, :].rearrange("p (i q) -> p i q", i=2)
                                    for i in range(2):
                                        pair, e = head_place(4 * g + 2 * n + i)
                                        last = pe.matmul(two[:, i, :], ks[:, pair, e, 0:keys], qs[:, pair, :],
                                                         start=i == 0, stop=first and a == "ca" and i == 1)
                                    if a == "sa":
                                        last = pe.matmul(two[:, :, 0:P], causal[:, :],
                                                         ident_r[:, :].rearrange("p (a q) -> p a q", a=1)
                                                         .to_broadcast([P, 2, P]), start=False, stop=True)
                                    elif masked:
                                        for u in range(QT):
                                            last = pe.matmul(two[:, :, u * P:(u + 1) * P], v["mask"][:, u, :],
                                                             ident_r[:, :].rearrange("p (a q) -> p a q", a=1)
                                                             .to_broadcast([P, 2, P]), start=False, stop=u == 1)
                                else:
                                    for i in range(4):
                                        pair, e = head_place(4 * g + i)
                                        pe.matmul(bank[:, i * P:(i + 1) * P], ks[:, pair, e, P:2 * P],
                                                  qs[:, pair, P:2 * P], start=i == 0, stop=False)
                                    last = pe.matmul(bank, causal[:, :],
                                                     ident_r[:, :].rearrange("p (a q) -> p a q", a=1)
                                                     .to_broadcast([P, 4, P]), start=False, stop=True)
                                last.then_inc(ring_ready.sem, 1)

                        def weighted(g):
                            if g == 0:
                                pe.wait_ge(v_ready.sem, v_ready.value(turn, (s, "v", a)))
                            if g % 2 == 0:
                                use = list(acc_freed[g // 2].events)
                                i = use.index(key)
                                before, back = (use[i - 1], 0) if i else (use[-1], 1)
                                pe.wait_ge(acc_freed[g // 2].sem, acc_freed[g // 2].value(turn, before, back))
                            pe.wait_ge(exp_ready.sem, exp_ready.value(turn, (*key, g, score_jobs(a) - 1)))
                            half = acc[:, g // 2, (g % 2) * SEQ:(g % 2 + 1) * SEQ]
                            for k in range(2 if a == "sa" else 1):
                                for j in range(4):
                                    if k == 0:
                                        moving = probs_of((*key, g))[0:keys, j * SEQ:(j + 1) * SEQ]
                                        out = half[32 * j:32 * j + 32, :]
                                    else:
                                        moving = probs_of((*key, g))[:, 4 * SEQ + j * P:4 * SEQ + (j + 1) * P]
                                        out = half[32 * j:32 * j + 32, P:2 * P]
                                    last = pe.matmul(out, v["v"][0:keys, k, 4 * g + j, :], moving, start=k == 0,
                                                     stop=k == 1 or a == "ca")
                            last.then_inc(probs_used.sem, 1)
                            if g % 2 == 1:
                                pe.wait_ge(probs_used.sem, probs_used.value(turn, (*key, g)))
                                pe.sem_inc(acc_ready[g // 2].sem, 1)

                        scores(0)
                        for g in range(GROUPS):
                            if g + 1 < GROUPS:
                                scores(g + 1)
                            weighted(g)
                    elif stage == "turned":
                        for b in range(2):
                            pe.wait_ge(heads_ready.sem, heads_ready.value(turn, (s, "attend", a, b)))
                        for u in range(QT):
                            bank = take_bank(turn, (*key, u))
                            for g in range(GROUPS):
                                last = pe.transpose(bank[:, g * P:(g + 1) * P], heads_out[:, g, u * P:(u + 1) * P],
                                                    ident[:, :])
                            last.then_inc(ring_ready.sem, 1)
                    elif stage == "o_proj":
                        w = f"{a}_o"
                        split_ready(turn, (s, "o_split", a))
                        bank = take_bank(turn, key)
                        for u in range(QT):
                            last = product(bank[:, u * D:(u + 1) * D],
                                           [[x[:, k, u * P:(u + 1) * P] for k in range(KT)]
                                            for x in (v["big_hi"], v["big_lo"])],
                                           [[x[:, k, :] for k in range(KT)] for x in (w_hi[w], w_lo[w])])
                        last.then_inc(ring_ready.sem, 1)
                    elif stage == "up":
                        if a == 0:
                            split_ready(turn, (s, "normal", ffn_ln))
                        bank = take_bank(turn, key)
                        for i in range(2):
                            m = 2 * a + i
                            last = product(bank[:, i * SEQ:(i + 1) * SEQ],
                                           [[x[:, k, m * P:(m + 1) * P] for k in range(KT)] for x in (w1_hi, w1_lo)],
                                           [[x[:, k, :] for k in range(KT)] for x in (v["ht_hi"], v["ht_lo"])])
                        last.then_inc(ring_ready.sem, 1)
                    elif stage == "down":
                        if a == 0:
                            use = list(acc_freed[s].events)
                            before = use[use.index((s, "down")) - 1]
                            pe.wait_ge(acc_freed[s].sem, acc_freed[s].value(turn, before))
                        split_ready(turn, (s, "up", a))
                        half = 2 * (a % 2)
                        for u in range(QT):
                            last = product(acc[:, s, u * D:(u + 1) * D],
                                           [[x[:, half + k, u * P:(u + 1) * P] for k in range(2)]
                                            for x in (v["big_hi"], v["big_lo"])],
                                           [[x[:, 2 * a + k, :] for k in range(2)] for x in (w2_hi, w2_lo)],
                                           start=a == 0 and u == 0, stop=a == 3 and u == 1)
                        if a == 3:
                            last.then_inc(acc_ready[s].sem, 1)


def program(nc, a):
    x = a["x"].rearrange("b n d -> (b n) d")
    ctx = a["ctx_1024"].rearrange("b n d -> (b n) d")
    mask = a["mask_BxSxS2_bk0"].rearrange("b n d -> (b n) d")
    out = a["out"].rearrange("b n d -> (b n) d")
    middle = nc.dram_tensor("middle", [BATCH * SEQ, D], F32).ap()
    l0, l1 = "L0_xattn_", "L1_xattn_"
    w0 = {f"{p}_{n}": a[f"{l0}{p}_w{n}"] for p in ("sa", "ca") for n in "qkvo"}
    w0.update(w1=a[l0 + "ffn_w1"], w2=a[l0 + "ffn_w2"])
    v0 = {f"{n}_{p}": a[f"{l0}{n}_{p}"] for n in ("ln1", "ln2", "ln3") for p in "gb"}
    v0.update(b1=a[l0 + "ffn_b1"], b2=a[l0 + "ffn_b2"])
    layer(nc, 0, x, ctx, None, middle, w0, v0)
    w1 = dict(ca_q=a[l1 + "q_w"], ca_k=a[l1 + "kv_w"][:, 0:D], ca_v=a[l1 + "kv_w"][:, D:2 * D],
              ca_o=a[l1 + "proj_w"], w1=a[l1 + "fc1_w"], w2=a[l1 + "fc2_w"])
    v1 = {f"{n}_{p}": a[f"{l1}{n}_{'w' if p == 'g' else 'b'}"] for n in ("cn", "qn", "n2") for p in "gb"}
    v1.update(b1=a[l1 + "fc1_b"], b2=a[l1 + "fc2_b"], proj_b=a[l1 + "proj_b"])
    layer(nc, 1, middle, ctx, mask, out, w1, v1)


def kernel(**inputs):
    import numpy as _np
    import concourse.bacc as _bacc
    from concourse import mybir as _mybir
    from concourse.bass_utils import run_bass_kernel_spmd as _run

    nc = _bacc.Bacc("TRN2", target_bir_lowering=False, num_devices=1)
    arrays, aps = {}, {}
    for name, value in inputs.items():
        a = _np.ascontiguousarray(value)
        arrays[f"in_{name}"] = a
        aps[name] = nc.dram_tensor(f"in_{name}", a.shape, _mybir.dt.from_np(a.dtype), kind="ExternalInput").ap()
    aps["out"] = nc.dram_tensor("out_0", (BATCH, SEQ, D), F32, kind="ExternalOutput").ap()
    program(nc, aps)
    r = _run(nc, [arrays], core_ids=[0])
    return r.results[0]["out_0"]
```

```python
import concourse.bass as bass
from concourse import mybir
from contextlib import ExitStack

F32 = mybir.dt.float32
F32R = mybir.dt.float32r
U8 = mybir.dt.uint8
ACT = mybir.ActivationFunctionType
ALU = mybir.AluOpType
AX = mybir.AxisListType

P = 128
BATCH = 64
SEQ = 256
CTX = 120
D = 256
FF = 1024
HEADS = 16
DK = D // HEADS
KT = D // P
QT = SEQ // P
PAIRS = HEADS // 2
PRODUCT_ROWS = 6 * DK
SCORE_ROWS = PRODUCT_ROWS + 2
GROUPS = 4
SLOTS = 2
PER_SLOT = BATCH // SLOTS
EPS = 1e-5
MASKED = -(2.0 ** 100)
RING = 3
FRING = 2
PRING = 2


def head_place(h):
    t, g = divmod(h, 8)
    return (g % 4) * 2 + t, g // 4


class Signal:

    def __init__(self, sem, events, step=1):
        self.sem, self.step, self.places = sem, step, {key: n for n, key in enumerate(events)}

    def start(self, engine):
        engine.sem_inc(self.sem, self.step * len(self.places))

    def value(self, seq, key, back=0):
        n = len(self.places)
        return seq.count(n * self.step, (n * (1 - back) + self.places[key] + 1) * self.step)


def ring_before(n, total, size):
    if n >= size:
        return n - size, 0
    last = total - 1 - (total - 1 - n) % size
    return last, 1


TIMES = [
    {"context": 0.5, "stats": 2.5, "normal": 1.0, "normal_t": 1.5, "split normal_t": 2.0, "q": 1.6, "k": 1.2,
     "v": 3.5, "max": 0.7, "c": 4.0, "scores": 1.8, "weighted": 0.4, "heads": 0.5, "turned": 1.4, "o_t": 1.2,
     "split o_t": 2.0, "o_proj": 2.5, "up": 1.6, "split up": 0.5, "down": 1.4, "down 3": 3.0},
    {"stats": 2.5, "normal": 1.0, "normal_t": 1.5, "split normal_t": 2.0, "q": 1.6, "k": 1.2,
     "v": 3.5, "max": 0.7, "c": 4.0, "scores": 1.4, "weighted": 0.4, "heads": 0.5, "turned": 1.4, "o_t": 1.2,
     "split o_t": 2.0, "o_proj": 2.5, "up": 1.6, "split up": 0.5, "down": 1.4, "down 3": 3.0},
]
CUT = [("prefetch",), ("c", "ca")]


def merge(one, two):
    def placed(slot, steps):
        total, at = sum(t for _, t in steps), 0.0
        for n, (step, t) in enumerate(steps):
            yield at / total, slot, n, step
            at += t
    return [(slot, step) for _, slot, _, step in sorted([*placed(0, one), *placed(1, two)], key=lambda x: x[:3])]


class Counts:

    def __init__(self, engine, turn, scratch):
        self.engine, self.turn, self.scratch, self.bases, self.n = engine, turn, scratch, {}, 0

    def value(self, factor, constant):
        if isinstance(self.turn, int):
            return self.turn * factor + constant
        base = self.bases[factor]
        self.n = (self.n + 1) % len(self.scratch)
        self.engine.reg_add(self.scratch[self.n], base, constant)
        return self.scratch[self.n]


class Seq:

    def __init__(self, counts, ahead=0):
        self.counts, self.ahead = counts, ahead

    def count(self, factor, constant):
        return self.counts.value(factor, self.ahead * factor + constant)

    def place(self, s):
        return self.counts.turn * SLOTS + (self.ahead * SLOTS + s)

    def next(self):
        return Seq(self.counts, self.ahead + 1)


class Slot:
    pass


def layer(nc, which, x_in, ctx_in, mask_in, x_out, weights, vectors):
    first = which == 0
    attentions = ["sa", "ca"] if first else ["ca"]
    masked = not first
    ffn_ln = "ln3" if first else "n2"
    ln_of = {"sa": "ln1", "ca": "ln2" if first else "qn"}

    def max_jobs(a):
        return 12 if a == "sa" else 8

    def score_jobs(a):
        return 3 if a == "sa" else 2

    def normalise(ln):
        return [("stats", ln), ("normal", ln), ("normal_t", ln), ("split", "normal_t", ln)]

    def attention(a):
        steps = [("q", a), ("split", "q", a), ("k", a), ("split", "k", a), ("v", a)]
        steps += [("max", a, n) for n in range(max_jobs(a))]
        steps += [("c", a)]
        score = [("scores", a, g) for g in range(GROUPS)]
        weighted = [("weighted", a, g) for g in range(GROUPS)]
        steps += [score[0], score[1], weighted[0], score[2], weighted[1], ("heads", a, 0), score[3],
                  weighted[2], ("turned", a, 0), weighted[3], ("heads", a, 1), ("turned", a, 1)]
        steps += [("o_t", a), ("split", "o_t", a), ("o_proj", a)]
        return steps

    feed_forward = []
    for i in range(4):
        feed_forward += [("up", i), ("split", "up", i)]
        if i:
            feed_forward += [("down", i - 1)]
    feed_forward += [("down", 3)]
    if first:
        steps = [("context",), ("split", "context")] + normalise("ln1") + attention("sa") + [("prefetch",)] + \
            normalise("ln2") + attention("ca") + normalise("ln3") + [("bias", "ln3")] + feed_forward
    else:
        steps = normalise("cn") + [("mask",)] + normalise("qn") + [("bias", "qn")] + attention("ca") + \
            [("prefetch",)] + normalise("n2") + [("bias", "n2")] + feed_forward
    times = [(step, TIMES[which].get(" ".join(map(str, step)), TIMES[which].get(" ".join(map(str, step[:2])),
              TIMES[which].get(step[0], 0.2)))) for step in steps]
    cut = steps.index(CUT[which])
    phase1, phase2 = times[:cut], times[cut:]

    ring_jobs = []
    for step in steps:
        if step[0] in ("context", "normal_t", "q", "k", "v", "o_t", "up", "max", "c", "turned", "o_proj"):
            ring_jobs.append(step)
        elif step[0] == "scores":
            ring_jobs += [(*step, n) for n in range(score_jobs(step[1]))]
    split_jobs = [step[1:] for step in steps if step[0] == "split"]
    groups = [step[1:] for step in steps if step[0] == "scores"]
    sums = [("heads", a, b) for a in attentions for b in range(2)] + [("down", 3)]
    lns = [step[1] for step in steps if step[0] == "stats"]

    stack = ExitStack()
    with stack:
        def sb(name, shape, dt):
            return stack.enter_context(nc.sbuf_tensor(f"L{which}_{name}", shape, dt))

        def semaphore(name):
            return stack.enter_context(nc.semaphore(f"L{which}_{name}"))

        names = [f"{a}_{n}" for a in attentions for n in "qkvo"]
        w_hi = {n: sb(f"{n}_hi", [P, KT, D], F32R) for n in names}
        w_lo = {n: sb(f"{n}_lo", [P, KT, D], F32R) for n in names}
        w1_hi, w1_lo = sb("w1_hi", [P, KT, FF], F32R), sb("w1_lo", [P, KT, FF], F32R)
        w2_hi, w2_lo = sb("w2_hi", [P, FF // P, D], F32R), sb("w2_lo", [P, FF // P, D], F32R)
        gain = {n: sb(f"{n}_gain", [P, KT], F32) for n in lns}
        shift = {n: sb(f"{n}_shift", [P, KT], F32) for n in lns}
        b1 = sb("b1", [P, FF // P], F32)
        b2 = sb("b2", [P, D], F32)
        proj_b = None if first else sb("proj_b", [P, D], F32)
        ident = sb("ident", [P, P], F32)
        ident_r = sb("ident_r", [P, P], F32R)
        causal = sb("causal", [P, P], F32R) if first else None
        minus_half = sb("minus_half", [P, QT], F32)
        ones_row = sb("ones_row", [1, SEQ], F32)
        split = sb("split", [P, SLOTS * FRING, 512], F32)
        staging = split[:, :, :].rearrange("p r n -> p (r n)")
        ring = stack.enter_context(nc.psum_tensor(f"L{which}_ring", [P, SLOTS * RING, 512], F32))
        acc = stack.enter_context(nc.psum_tensor(f"L{which}_acc", [P, SLOTS, 512], F32))

        w_loaded = semaphore("w_loaded")
        w_lead = semaphore("w_lead")
        w_split = semaphore("w_split")
        vec_loaded = semaphore("vec_loaded")
        cleared = semaphore("cleared")
        built = semaphore("built")
        ones_set = semaphore("ones_set")
        pads_set = semaphore("pads_set")
        stats_seen = semaphore("stats_seen")

        slots, multiples = [], set()
        for s in range(SLOTS):
            v = Slot()
            slots.append(v)
            v.xin = sb(f"xin{s}", [P, QT, D], F32)
            v.x = sb(f"x{s}", [P, QT, D], F32)
            v.z = sb(f"z{s}", [P, QT, D], F32)
            v.cin = sb(f"cin{s}", [CTX, D], F32)
            v.cz = None if first else sb(f"cz{s}", [CTX, D], F32)
            v.ht_hi, v.ht_lo = (sb(f"ht_{h}{s}", [P, KT, SEQ], F32R) for h in ("hi", "lo"))
            v.ct_hi, v.ct_lo = (sb(f"ct_{h}{s}", [P, KT, CTX], F32R) for h in ("hi", "lo"))
            v.big_hi, v.big_lo = (sb(f"big_{h}{s}", [P, 4 * SEQ], F32R) for h in ("hi", "lo"))
            v.v = sb(f"v{s}", [P, 2 if first else 1, HEADS, 32], F32)
            v.qs = sb(f"qs{s}", [P, PAIRS, SEQ], F32R)
            v.ks = sb(f"ks{s}", [P, PAIRS, 2, SEQ if first else CTX], F32R)
            v.neg = sb(f"neg{s}", [P, QT, P], F32)
            v.c = sb(f"c{s}", [HEADS, SEQ], F32R)
            v.probs = sb(f"probs{s}", [P, PRING, 4 * 384 if first else 4 * SEQ], F32)
            v.heads = sb(f"heads{s}", [P, 2, SEQ], F32)
            v.stats = sb(f"stats{s}", [P, QT, 6], F32)
            v.mv = sb(f"mv{s}", [P, QT, 2], F32)
            v.rstd = sb(f"rstd{s}", [P, QT], F32)
            v.rden = sb(f"rden{s}", [P, 2, QT, 8], F32)
            v.mask8 = None if first else sb(f"mask8{s}", [P, QT, CTX], U8)
            v.mask = None if first else sb(f"mask{s}", [P, QT, CTX], F32R)
            v.ring = ring[:, RING * s:RING * (s + 1), :]
            v.acc = acc[:, s, :]
            v.split = split[:, FRING * s:FRING * (s + 1), :]

            def signal(name, events, step=1):
                if events:
                    multiples.add(len(events) * step)
                return Signal(semaphore(f"{name}{s}"), events, step)

            halves = [(a, b) for a in attentions for b in range(2)]
            v.ring_ready = signal("ring_ready", ring_jobs)
            v.maxed = signal("maxed", [j[1:] for j in ring_jobs if j[0] == "max"])
            v.exp_done = signal("exp_done", [j[1:] for j in ring_jobs if j[0] == "scores"])
            v.f_ready = signal("f_ready", split_jobs)
            v.hi_ready = signal("hi_ready", split_jobs)
            v.lo_ready = signal("lo_ready", split_jobs)
            v.v_ready = signal("v_ready", attentions)
            v.c_ready = signal("c_ready", attentions)
            v.probs_used = signal("probs_used", groups)
            v.down_ready = signal("down_ready", ["ffn"])
            v.heads_ready = signal("heads_ready", halves)
            v.rden_ready = signal("rden_ready", halves)
            v.oq_ready = signal("oq_ready", halves)
            v.x_ready = signal("x_ready", [*attentions, "ffn"])
            v.stats_ready = signal("stats_ready", lns)
            v.mv_ready = signal("mv_ready", lns)
            v.eps_ready = signal("eps_ready", lns)
            v.rstd_ready = signal("rstd_ready", lns)
            v.z_ready = signal("z_ready", lns)
            v.bias_ready = signal("bias_ready", [ffn_ln] if first else ["qn", ffn_ln])
            v.mask_ready = signal("mask_ready", ["mask"] if masked else [])
            v.xin_loaded = signal("xin_loaded", ["x"], 16)
            v.cin_loaded = signal("cin_loaded", ["c"], 16)
            v.mask_loaded = signal("mask_loaded", ["m"] if masked else [], 16)
            v.q_loaded = signal("q_loaded", [(a, n) for a in attentions for n in range(3)], 16)
            v.k_loaded = signal("k_loaded", [(a, n) for a in attentions for n in range(6)], 16)
            v.c_loaded = signal("c_loaded", attentions, 16)
            v.stored = signal("stored", ["x"], 16)

        def bank_of(v, job):
            return v.ring[:, ring_jobs.index(job) % RING, :]

        def tile_of(v, job):
            return v.split[:, split_jobs.index(job) % FRING, :]

        def reading_done(v, job):
            if job in split_jobs:
                return v.f_ready, job
            if job == ("down", 3):
                return v.x_ready, "ffn"
            return {"v": (v.v_ready, job[1]), "max": (v.maxed, job[1:]), "c": (v.c_ready, job[1]),
                    "scores": (v.exp_done, job[1:]), "turned": (v.oq_ready, job[1:]),
                    "heads": (v.heads_ready, job[1:]), "o_proj": (v.x_ready, job[1])}[job[0]]

        def probs_of(v, group):
            return v.probs[:, groups.index(group) % PRING, :]

        def keys_of(a):
            return SEQ if a == "sa" else CTX

        def split_to(v, job):
            if job[0] == "context" or job[-1] == "cn":
                return (v.ct_hi[:, :, :].rearrange("p k n -> p (k n)"),
                        v.ct_lo[:, :, :].rearrange("p k n -> p (k n)"), KT * CTX)
            if job[0] == "normal_t":
                return (v.ht_hi[:, :, :].rearrange("p k n -> p (k n)"),
                        v.ht_lo[:, :, :].rearrange("p k n -> p (k n)"), KT * SEQ)
            half = {"q": 0, "k": 1, "o_t": 0}[job[0]] if job[0] != "up" else job[1] % 2
            width = KT * keys_of(job[1]) if job[0] == "k" else 2 * SEQ
            at = slice(2 * SEQ * half, 2 * SEQ * half + width)
            return v.big_hi[:, at], v.big_lo[:, at], width

        def in_both_slots(engine, step):
            last = Seq(Counts(engine, PER_SLOT - 1, None))
            for what, _ in phase1:
                step(0, Seq(Counts(engine, 0, None)), what)
            with ExitStack() as registers:
                scratch = [registers.enter_context(engine.register(f"L{which}_wait{n}")) for n in range(4)]
                bases = {k: registers.enter_context(engine.register(f"L{which}_times{k}")) for k in sorted(multiples)}
                with engine.Fori(0, PER_SLOT - 1) as turn:
                    counts = Counts(engine, turn, scratch)
                    counts.bases = bases
                    for k, register in bases.items():
                        engine.reg_mov(register, turn * k)
                    for s, what in merge(phase2, phase1):
                        step(s, Seq(counts), what)
                    for s, what in merge(phase1, phase2):
                        step(s, Seq(counts, 1 if s == 0 else 0), what)
            for s, what in merge(phase2, phase1):
                step(s, last, what, ending=True)
            for what, _ in phase2:
                step(1, last, what, ending=True)

        loads = []
        for n in names:
            loads.append((n, weights[n].rearrange("(k p) n -> p k n", p=P), KT, D, w_hi[n], w_lo[n]))
        loads.append(("w1", weights["w1"].rearrange("(k p) n -> p k n", p=P), KT, FF, w1_hi, w1_lo))
        loads.append(("w2", weights["w2"].rearrange("(k p) n -> p k n", p=P), FF // P, D, w2_hi, w2_lo))
        vector_loads = [(gain[n], vectors[n + "_g"]) for n in lns] + \
            [(shift[n], vectors[n + "_b"]) for n in lns] + [(b1, vectors["b1"])]
        row_loads = [(b2, vectors["b2"])] + ([] if first else [(proj_b, vectors["proj_b"])])
        all_vectors = 16 * (len(vector_loads) + len(row_loads))

        block = stack.enter_context(nc.Block())

        @block.sync
        def _(sp):
            with nc.allow_non_contiguous_dma(reason="one value per partition, once"):
                for dst, src in vector_loads:
                    sp.dma_start(dst[:, :], src.rearrange("(k p) -> p k", p=P)).then_inc(vec_loaded, 16)
            for dst, src in row_loads:
                sp.dma_start(dst[:, :], src.rearrange("(a n) -> a n", a=1).to_broadcast([P, D]))\
                    .then_inc(vec_loaded, 16)
            for n, (_, src, kt, width, _, _) in enumerate(loads):
                if n:
                    sp.wait_ge(w_split, n)
                sp.dma_start(staging[:, 0:kt * width].rearrange("p (k n) -> p k n", k=kt), src)\
                    .then_inc(w_loaded, 16)
            sp.wait_ge(cleared, 1)
            sp.wait_ge(ones_set, 1)
            keys = SEQ if first else CTX
            for v in slots:
                for e in range(2):
                    sp.dma_start(v.ks[PRODUCT_ROWS + e:PRODUCT_ROWS + e + 1, :, e, :].bitcast(F32),
                                 ones_row[0:1, 0:keys].rearrange("a (k n) -> a k n", k=1)
                                 .to_broadcast([1, PAIRS, keys])).then_inc(pads_set, 16)
            for v in slots:
                for sig in (v.xin_loaded, v.cin_loaded, v.mask_loaded, v.q_loaded, v.k_loaded, v.c_loaded, v.stored):
                    if sig.places:
                        sig.start(sp)

            def load(s, seq, free=None):
                v = slots[s]
                token, row = seq.place(s) * SEQ, seq.place(s) * CTX
                if free:
                    token, row = sp.snap(token), sp.snap(row)
                    sp.wait_ge(*free)
                sp.dma_start(v.xin[:, :, :], x_in[bass.ds(token, SEQ), :]
                             .rearrange("(u p) d -> p u d", p=P)).then_inc(v.xin_loaded.sem, 16)
                sp.dma_start(v.cin[:, :], ctx_in[bass.ds(row, CTX), :]).then_inc(v.cin_loaded.sem, 16)
                if masked:
                    sp.dma_start(v.mask8[:, :, :], mask_in[bass.ds(token, SEQ), :]
                                 .rearrange("(u p) d -> p u d", p=P)).then_inc(v.mask_loaded.sem, 16)

            def step(s, seq, what, ending=False):
                v = slots[s]
                if what == ("prefetch",) and not ending:
                    load(s, seq.next(), (v.x_ready.sem, v.x_ready.value(seq, attentions[0])))
                elif what[0] == "split" and what[1] == "q":
                    for c, part in ((0, v.big_hi), (2, v.big_hi), (1, v.big_lo)):
                        signal = v.lo_ready if part is v.big_lo else v.hi_ready
                        if c != 2:
                            sp.wait_ge(signal.sem, signal.value(seq, what[1:]))
                        sp.dma_start(v.qs[32 * c:32 * c + 32, :, :].bitcast(F32), part[:, 0:2 * SEQ].bitcast(F32))\
                            .then_inc(v.q_loaded.sem, 16)
                elif what[0] == "split" and what[1] == "k":
                    n = keys_of(what[2])
                    for c, part in ((0, v.big_hi), (1, v.big_hi), (2, v.big_lo)):
                        signal = v.lo_ready if part is v.big_lo else v.hi_ready
                        if c != 1:
                            sp.wait_ge(signal.sem, signal.value(seq, what[1:]))
                        for e in range(2):
                            row = 32 * c + DK * e
                            src = part[P // 2 * e:P // 2 * (e + 1), 2 * SEQ:2 * SEQ + 2 * n]\
                                .rearrange("p (k n) -> p k n", k=KT)
                            sp.dma_start(v.ks[row:row + DK, :, e, 0:n].bitcast(F32), src.bitcast(F32))\
                                .then_inc(v.k_loaded.sem, 16)
                elif what[0] == "c":
                    sp.wait_ge(v.c_ready.sem, v.c_ready.value(seq, what[1]))
                    sp.dma_start(v.qs[PRODUCT_ROWS:SCORE_ROWS, :, :].bitcast(F32), v.c[:, :].bitcast(F32))\
                        .then_inc(v.c_loaded.sem, 16)
                elif what == ("down", 3):
                    token = sp.snap(seq.place(s) * SEQ)
                    sp.wait_ge(v.x_ready.sem, v.x_ready.value(seq, "ffn"))
                    sp.dma_start(x_out[bass.ds(token, SEQ), :]
                                 .rearrange("(u p) d -> p u d", p=P), v.x[:, :, :]).then_inc(v.stored.sem, 16)

            for s in range(SLOTS):
                load(s, Seq(Counts(sp, 0, None)))
            in_both_slots(sp, step)
            for v in slots:
                sp.wait_ge(v.stored.sem, 16 * (PER_SLOT + 1))

        @block.gpsimd
        def _(pool):
            pool.memset(ident[:, :], 0.0).then_inc(built, 1)
            pool.memset(minus_half[:, :], -0.5)
            pool.memset(ones_row[:, :], 1.0).then_inc(ones_set, 1)
            pool.wait_ge(built, 1)
            pool.affine_select(out=ident[:, :], in_=ident[:, :], compare_op=ALU.not_equal, fill=1.0,
                               base=0, pattern=[[-1, P]], channel_multiplier=1).then_inc(built, 1)
            for v in slots:
                for sig in (v.lo_ready, v.rstd_ready, v.bias_ready):
                    sig.start(pool)
            pool.wait_ge(vec_loaded, all_vectors)

            def step(s, seq, what, ending=False):
                v = slots[s]
                if what[0] == "stats":
                    rows, us = (CTX, 1) if what[1] == "cn" else (P, QT)
                    pool.wait_ge(v.eps_ready.sem, v.eps_ready.value(seq, what[1]))
                    pool.tensor_tensor(v.rstd[0:rows, 0:us], v.rstd[0:rows, 0:us], minus_half[0:rows, 0:us],
                                       ALU.pow).then_inc(v.rstd_ready.sem, 1)
                elif what[0] == "split":
                    hi, lo, width = split_to(v, what[1:])
                    pool.wait_ge(v.hi_ready.sem, v.hi_ready.value(seq, what[1:]))
                    pool.tensor_tensor(lo, tile_of(v, what[1:])[:, 0:width], hi.bitcast(F32), ALU.subtract)\
                        .then_inc(v.lo_ready.sem, 1)
                elif what[0] == "bias":
                    src, row = (v.x, b2) if what[1] == ffn_ln else (v.xin, proj_b)
                    pool.wait_ge(v.z_ready.sem, v.z_ready.value(seq, what[1]))
                    pool.tensor_tensor(src[:, :, :], src[:, :, :],
                                       row[:, :].rearrange("p (a n) -> p a n", a=1).to_broadcast([P, QT, D]),
                                       ALU.add).then_inc(v.bias_ready.sem, 1)

            in_both_slots(pool, step)

        @block.scalar
        def _(act):
            for v in slots:
                for sig in (v.f_ready, v.v_ready, v.exp_done, v.heads_ready):
                    sig.start(act)
            act.wait_ge(vec_loaded, all_vectors)
            act.wait_ge(w_split, len(loads))
            act.wait_ge(cleared, 1)

            def step(s, seq, what, ending=False):
                v = slots[s]
                if what in split_jobs:
                    bank, tile, width = bank_of(v, what), tile_of(v, what), split_to(v, what)[2]
                    act.wait_ge(v.ring_ready.sem, v.ring_ready.value(seq, what))
                    before, back = ring_before(split_jobs.index(what), len(split_jobs), FRING)
                    act.wait_ge(v.lo_ready.sem, v.lo_ready.value(seq, split_jobs[before], back))
                    half = width // 2
                    if what[0] == "normal_t":
                        for k in range(KT):
                            last = act.activation(tile[:, k * half:(k + 1) * half], bank[:, k * half:(k + 1) * half],
                                                  ACT.Identity, bias=shift[what[1]][:, k:k + 1],
                                                  scale=gain[what[1]][:, k:k + 1])
                    elif what[0] == "up":
                        for m in range(2):
                            last = act.activation(tile[:, m * half:(m + 1) * half], bank[:, m * half:(m + 1) * half],
                                                  ACT.Relu if first else ACT.Gelu,
                                                  bias=b1[:, 2 * what[1] + m:2 * what[1] + m + 1])
                    else:
                        last = act.activation(tile[:, 0:width], bank[:, 0:width], ACT.Copy,
                                              scale=DK ** -0.5 if what[0] == "k" else 1.0)
                    last.then_inc(v.f_ready.sem, 1)
                elif what[0] == "v":
                    act.wait_ge(v.ring_ready.sem, v.ring_ready.value(seq, what))
                    rows, tiles = (P, 2) if what[1] == "sa" else (CTX, 1)
                    for k in range(tiles):
                        last = act.activation(
                            v.v[0:rows, k, :, 0:DK],
                            bank_of(v, what)[0:rows, k * D:(k + 1) * D].rearrange("p (h d) -> p h d", d=DK), ACT.Copy)
                    last.then_inc(v.v_ready.sem, 1)
                elif what[0] == "scores":
                    a, g = what[1:]
                    rows = P if a == "sa" else CTX
                    before, back = ring_before(groups.index((a, g)), len(groups), PRING)
                    act.wait_ge(v.probs_used.sem, v.probs_used.value(seq, groups[before], back))
                    for n in range(score_jobs(a)):
                        act.wait_ge(v.ring_ready.sem, v.ring_ready.value(seq, (*what, n)))
                        act.activation(probs_of(v, (a, g))[0:rows, 512 * n:512 * n + 512],
                                       bank_of(v, (*what, n))[0:rows, :], ACT.Exp).then_inc(v.exp_done.sem, 1)
                elif what[0] == "heads":
                    act.wait_ge(v.probs_used.sem, v.probs_used.value(seq, (what[1], 2 * what[2] + 1)))
                    act.activation(v.heads[:, :, :].rearrange("p g n -> p (g n)"), v.acc, ACT.Copy)\
                        .then_inc(v.heads_ready.sem, 1)

            in_both_slots(act, step)

        @block.vector
        def _(dve):
            for v in slots:
                dve.memset(v.qs[:, :, :].bitcast(F32), 0.0)
                dve.memset(v.ks[:, :, :, :].bitcast(F32), 0.0)
                dve.memset(v.v[:, :, :, DK:32], 0.0)
                last = dve.memset(v.neg[:, :, :], 0.0)
            last.then_inc(w_lead, 1)
            dve.wait_ge(w_lead, 1)
            for v in slots:
                last = dve.memset(v.v[:, :, :, DK:DK + 1], 1.0)
            last.then_inc(cleared, 1)
            for n, (name, _, kt, width, hi, lo) in enumerate(loads):
                dve.wait_ge(w_loaded, 16 * (n + 1))
                src = staging[:, 0:kt * width]
                hi, lo = (x[:, :, :].rearrange("p k n -> p (k n)") for x in (hi, lo))
                if name[-2:] in ("_q", "_k"):
                    src = src.rearrange("p (k j d) -> p k d j", k=kt * KT * 2, d=DK)
                    hi, lo = (x.rearrange("p (k d j) -> p k d j", k=kt * KT * 2, d=DK) for x in (hi, lo))
                dve.tensor_copy(hi, src).then_inc(w_lead, 1)
                dve.wait_ge(w_lead, n + 2)
                dve.tensor_tensor(lo, src, hi.bitcast(F32), ALU.subtract).then_inc(w_split, 1)
            dve.wait_ge(built, 2)
            dve.tensor_copy(ident_r[:, :], ident[:, :]).then_inc(built, 1)
            if first:
                later = slots[0].z[:, 0, 0:P]
                dve.tensor_tensor_scan(later, ident[:, :], ident[:, :], 0.0, ALU.max, ALU.max).then_inc(built, 1)
                dve.wait_ge(built, 4)
                dve.tensor_tensor(later, later, ident[:, :], ALU.subtract).then_inc(built, 1)
                dve.wait_ge(built, 5)
                dve.tensor_scalar(causal[:, :], later, MASKED, None, ALU.mult).then_inc(built, 1)
            for v in slots:
                for sig in (v.maxed, v.hi_ready, v.c_ready, v.rden_ready, v.oq_ready, v.x_ready,
                            v.stats_ready, v.mv_ready, v.eps_ready, v.z_ready, *([v.mask_ready] if masked else [])):
                    sig.start(dve)

            def source(v, ln):
                if ln == "cn":
                    return v.cin[:, :].rearrange("p (u d) -> p u d", u=1)
                return v.xin if ln in ("ln1", "qn") else v.x

            def step(s, seq, what, ending=False):
                v = slots[s]
                if what[0] == "stats":
                    ln = what[1]
                    rows, us = (CTX, 1) if ln == "cn" else (P, QT)
                    if ln == "cn":
                        dve.wait_ge(v.cin_loaded.sem, v.cin_loaded.value(seq, "c"))
                    elif ln in ("ln1", "qn"):
                        dve.wait_ge(v.xin_loaded.sem, v.xin_loaded.value(seq, "x"))
                    else:
                        dve.wait_ge(v.x_ready.sem, v.x_ready.value(seq, "sa" if ln == "ln2" else "ca"))
                    for u in range(us):
                        last = dve.bn_stats(v.stats[0:rows, u, :], source(v, ln)[:, u, :])
                    last.then_inc(v.stats_ready.sem, 1)
                    dve.wait_ge(v.stats_ready.sem, v.stats_ready.value(seq, ln))
                    dve.sem_inc(stats_seen, 1)
                    for u in range(us):
                        last = dve.bn_aggr(v.mv[0:rows, u, :], v.stats[0:rows, u, :])
                    last.then_inc(v.mv_ready.sem, 1)
                    dve.wait_ge(v.mv_ready.sem, v.mv_ready.value(seq, ln))
                    dve.tensor_scalar(v.rstd[0:rows, 0:us], v.mv[0:rows, 0:us, 1], EPS, None, ALU.add)\
                        .then_inc(v.eps_ready.sem, 1)
                elif what[0] == "mask":
                    dve.wait_ge(v.mask_loaded.sem, v.mask_loaded.value(seq, "m"))
                    dve.tensor_scalar(v.mask[:, :, :], v.mask8[:, :, :], MASKED, None, ALU.mult)\
                        .then_inc(v.mask_ready.sem, 1)
                elif what[0] == "normal":
                    ln = what[1]
                    rows, us = (CTX, 1) if ln == "cn" else (P, QT)
                    dst = v.cz[:, :].rearrange("p (u d) -> p u d", u=1) if ln == "cn" else v.z
                    dve.wait_ge(v.rstd_ready.sem, v.rstd_ready.value(seq, ln))
                    for u in range(us):
                        last = dve.tensor_scalar(dst[:, u, :], source(v, ln)[:, u, :], v.mv[0:rows, u, 0:1],
                                                 v.rstd[0:rows, u:u + 1], ALU.subtract, ALU.mult)
                    last.then_inc(v.z_ready.sem, 1)
                elif what[0] == "split":
                    hi, _, width = split_to(v, what[1:])
                    dve.wait_ge(v.f_ready.sem, v.f_ready.value(seq, what[1:]))
                    dve.tensor_copy(hi, tile_of(v, what[1:])[:, 0:width]).then_inc(v.hi_ready.sem, 1)
                elif what[0] == "max":
                    a, n = what[1:]
                    dve.wait_ge(v.ring_ready.sem, v.ring_ready.value(seq, what))
                    neg = v.neg[:, :, 0:HEADS].rearrange("p u (e r) -> p u r e", e=2)
                    if a == "ca":
                        out = neg[:, :, n, :]
                        scores = bank_of(v, what)[:, 0:QT * 2 * CTX].rearrange("p (u e k) -> p u e k", u=QT, e=2)
                    elif n < PAIRS:
                        out = neg[:, 1, n, :]
                        scores = bank_of(v, what).rearrange("p (e k) -> p e k", e=2)
                    else:
                        out = neg[:, 0, 2 * (n - PAIRS):2 * (n - PAIRS) + 2, :]
                        scores = bank_of(v, what).rearrange("p (r e k) -> p r e k", r=2, e=2)
                    dve.tensor_reduce(out, scores, AX.X, ALU.max, negate=True).then_inc(v.maxed.sem, 1)
                elif what[0] == "c":
                    dve.wait_ge(v.ring_ready.sem, v.ring_ready.value(seq, what))
                    dve.tensor_copy(v.c[:, :], bank_of(v, what)[0:HEADS, 0:SEQ]).then_inc(v.c_ready.sem, 1)
                elif what[0] == "turned":
                    a, b = what[1:]
                    dve.wait_ge(v.ring_ready.sem, v.ring_ready.value(seq, what))
                    o = bank_of(v, what).rearrange("p (u h c) -> p u h c", u=QT, c=32)
                    dve.reciprocal(v.rden[:, b, :, :], o[:, :, :, DK]).then_inc(v.rden_ready.sem, 1)
                    dve.wait_ge(v.rden_ready.sem, v.rden_ready.value(seq, (a, b)))
                    for u in range(QT):
                        last = dve.tensor_tensor(
                            v.z[:, u, b * P:(b + 1) * P].rearrange("p (h d) -> p h d", d=DK), o[:, u, :, 0:DK],
                            v.rden[:, b, u, :].rearrange("p (h d) -> p h d", d=1).to_broadcast([P, 8, DK]), ALU.mult)
                    last.then_inc(v.oq_ready.sem, 1)
                elif what[0] == "o_proj":
                    a = what[1]
                    src = v.xin if a == attentions[0] else v.x
                    if a == attentions[0]:
                        dve.wait_ge(v.stored.sem, v.stored.value(seq, "x", 1))
                    if masked:
                        dve.wait_ge(v.bias_ready.sem, v.bias_ready.value(seq, "qn"))
                    dve.wait_ge(v.ring_ready.sem, v.ring_ready.value(seq, what))
                    dve.tensor_tensor(v.x[:, :, :].rearrange("p u d -> p (u d)"), bank_of(v, what),
                                      src[:, :, :].rearrange("p u d -> p (u d)"), ALU.add).then_inc(v.x_ready.sem, 1)
                elif what == ("down", 3):
                    dve.wait_ge(v.bias_ready.sem, v.bias_ready.value(seq, ffn_ln))
                    dve.wait_ge(v.down_ready.sem, v.down_ready.value(seq, "ffn"))
                    x = v.x[:, :, :].rearrange("p u d -> p (u d)")
                    dve.tensor_tensor(x, v.acc, x, ALU.add).then_inc(v.x_ready.sem, 1)

            in_both_slots(dve, step)

        @block.tensor
        def _(pe):
            for v in slots:
                for sig in (v.ring_ready, v.probs_used, v.down_ready):
                    sig.start(pe)
            pe.wait_ge(w_split, len(loads))
            pe.wait_ge(built, 6 if first else 3)
            pe.wait_ge(pads_set, 16 * 2 * SLOTS)

            def take_bank(v, seq, job):
                before, back = ring_before(ring_jobs.index(job), len(ring_jobs), RING)
                done, event = reading_done(v, ring_jobs[before])
                pe.wait_ge(done.sem, done.value(seq, event, back))
                return bank_of(v, job)

            def take_sum(v, seq, key):
                before, back = ring_before(sums.index(key), len(sums), 1)
                done, event = reading_done(v, sums[before])
                pe.wait_ge(done.sem, done.value(seq, event, back))

            def product(out, stationary, moving, start=True, stop=True):
                tiles = len(stationary[0])
                for k in range(tiles):
                    for i, (x, y) in enumerate(((0, 0), (1, 0), (0, 1))):
                        last = pe.matmul(out, stationary[x][k], moving[y][k], start=start and k == 0 and i == 0,
                                         stop=stop and k == tiles - 1 and i == 2)
                return last

            def columns(pair, at, n, tiles=KT):
                return [[x[:, k, at:at + n] for k in range(tiles)] for x in pair]

            def repeated(tile, times, n=P):
                return tile.rearrange("p (a q) -> p a q", a=1).to_broadcast([P, times, n])

            def split_ready(v, seq, *job):
                pe.wait_ge(v.lo_ready.sem, v.lo_ready.value(seq, job))

            def step(s, seq, what, ending=False):
                v = slots[s]
                a = what[1] if len(what) > 1 else None
                ht, ct = (v.ht_hi, v.ht_lo), (v.ct_hi, v.ct_lo)
                if what[0] == "context" or what == ("normal_t", "cn"):
                    if first:
                        src = v.cin
                        pe.wait_ge(v.cin_loaded.sem, v.cin_loaded.value(seq, "c"))
                    else:
                        src = v.cz
                        pe.wait_ge(v.z_ready.sem, v.z_ready.value(seq, "cn"))
                    bank = take_bank(v, seq, what)
                    for k in range(KT):
                        last = pe.transpose(bank[:, k * CTX:(k + 1) * CTX], src[:, k * P:(k + 1) * P],
                                            ident[0:CTX, 0:CTX])
                    last.then_inc(v.ring_ready.sem, 1)
                elif what[0] in ("normal_t", "o_t"):
                    if what[0] == "normal_t":
                        pe.wait_ge(v.z_ready.sem, v.z_ready.value(seq, a))
                    else:
                        pe.wait_ge(v.oq_ready.sem, v.oq_ready.value(seq, (a, 1)))
                    bank = take_bank(v, seq, what)
                    for k in range(KT):
                        for u in range(QT):
                            last = pe.transpose(bank[:, (k * QT + u) * P:(k * QT + u + 1) * P],
                                                v.z[:, u, k * P:(k + 1) * P], ident[:, :])
                    last.then_inc(v.ring_ready.sem, 1)
                elif what[0] in ("q", "k"):
                    if what[0] == "q":
                        split_ready(v, seq, "normal_t", ln_of[a])
                    elif a == "ca":
                        split_ready(v, seq, *(("context",) if first else ("normal_t", "cn")))
                    n, tokens = (SEQ, ht) if what[0] == "q" or a == "sa" else (CTX, ct)
                    w = f"{a}_{what[0]}"
                    bank = take_bank(v, seq, what)
                    for t in range(KT):
                        last = product(bank[:, t * n:(t + 1) * n], columns((w_hi[w], w_lo[w]), t * P, P),
                                       columns(tokens, 0, n))
                    last.then_inc(v.ring_ready.sem, 1)
                elif what[0] == "v":
                    tokens, tiles, rows = (ht, 2, P) if a == "sa" else (ct, 1, CTX)
                    w = f"{a}_v"
                    bank = take_bank(v, seq, what)
                    for u in range(tiles):
                        last = product(bank[0:rows, u * D:(u + 1) * D], columns(tokens, u * P, rows),
                                       columns((w_hi[w], w_lo[w]), 0, D))
                    last.then_inc(v.ring_ready.sem, 1)
                elif what[0] == "max":
                    n = what[2]
                    qs, ks = v.qs[0:PRODUCT_ROWS, :, :], v.ks[0:PRODUCT_ROWS, :, :, :]
                    if n == 0:
                        pe.wait_ge(v.q_loaded.sem, v.q_loaded.value(seq, (a, 2)))
                        pe.wait_ge(v.k_loaded.sem, v.k_loaded.value(seq, (a, 5)))
                        if masked:
                            pe.wait_ge(v.mask_ready.sem, v.mask_ready.value(seq, "mask"))
                    bank = take_bank(v, seq, what)
                    if a == "ca":
                        halves = [bank[:, u * 2 * CTX:(u + 1) * 2 * CTX] for u in range(QT)]
                        for u in range(QT):
                            last = pe.matmul(halves[u], qs[:, n, u * P:(u + 1) * P], ks[:, n, :, 0:CTX],
                                             start=u == 0, stop=not masked and u == 1)
                        for u in range(QT if masked else 0):
                            last = pe.matmul(halves[u], ident_r[:, :], v.mask[:, u:u + 1, :].to_broadcast([P, 2, CTX]),
                                             start=False, stop=u == 1)
                    elif n < PAIRS:
                        pe.matmul(bank, qs[:, n, P:2 * P], ks[:, n, :, :], start=True, stop=False)
                        last = pe.matmul(bank.rearrange("p (e k) -> p e k", e=2)[:, :, P:2 * P], ident_r[:, :],
                                         repeated(causal[:, :], 2), start=False, stop=True)
                    else:
                        for i in range(2):
                            pair = 2 * (n - PAIRS) + i
                            pe.matmul(bank[:, i * 2 * P:(i + 1) * 2 * P], qs[:, pair, 0:P], ks[:, pair, :, 0:P],
                                      start=i == 0, stop=False)
                        last = pe.matmul(bank, ident_r[:, :], repeated(causal[:, :], 4), start=False, stop=True)
                    last.then_inc(v.ring_ready.sem, 1)
                elif what[0] == "c":
                    pe.wait_ge(v.maxed.sem, v.maxed.value(seq, (a, max_jobs(a) - 1)))
                    bank = take_bank(v, seq, what)
                    for u in range(QT):
                        last = pe.transpose(bank[:, u * P:(u + 1) * P], v.neg[:, u, :], ident[:, :])
                    last.then_inc(v.ring_ready.sem, 1)
                elif what[0] == "scores":
                    g = what[2]
                    keys = P if a == "sa" else CTX
                    qs, ks = v.qs[0:SCORE_ROWS, :, :], v.ks[0:SCORE_ROWS, :, :, :]
                    if g == 0:
                        pe.wait_ge(v.c_loaded.sem, v.c_loaded.value(seq, a))
                    for n in range(score_jobs(a)):
                        bank = take_bank(v, seq, (*what, n))
                        if n < 2:
                            two = bank[0:keys, :].rearrange("p (i q) -> p i q", i=2)
                            for i in range(2):
                                pair, e = head_place(4 * g + 2 * n + i)
                                last = pe.matmul(two[:, i, :], ks[:, pair, e, 0:keys], qs[:, pair, :],
                                                 start=i == 0, stop=first and a == "ca" and i == 1)
                            if a == "sa":
                                last = pe.matmul(two[:, :, 0:P], causal[:, :], repeated(ident_r[:, :], 2),
                                                 start=False, stop=True)
                            elif masked:
                                for u in range(QT):
                                    last = pe.matmul(two[:, :, u * P:(u + 1) * P], v.mask[:, u, :],
                                                     repeated(ident_r[:, :], 2), start=False, stop=u == 1)
                        else:
                            for i in range(4):
                                pair, e = head_place(4 * g + i)
                                pe.matmul(bank[:, i * P:(i + 1) * P], ks[:, pair, e, P:2 * P], qs[:, pair, P:2 * P],
                                          start=i == 0, stop=False)
                            last = pe.matmul(bank, causal[:, :], repeated(ident_r[:, :], 4), start=False, stop=True)
                        last.then_inc(v.ring_ready.sem, 1)
                elif what[0] == "weighted":
                    g = what[2]
                    keys = P if a == "sa" else CTX
                    if g == 0:
                        pe.wait_ge(v.v_ready.sem, v.v_ready.value(seq, a))
                    if g % 2 == 0:
                        take_sum(v, seq, ("heads", a, g // 2))
                    pe.wait_ge(v.exp_done.sem, v.exp_done.value(seq, (a, g, score_jobs(a) - 1)))
                    half = v.acc[:, (g % 2) * SEQ:(g % 2 + 1) * SEQ]
                    probs = probs_of(v, (a, g))
                    for k in range(2 if a == "sa" else 1):
                        for j in range(4):
                            if k == 0:
                                moving, out = probs[0:keys, j * SEQ:(j + 1) * SEQ], half[32 * j:32 * j + 32, :]
                            else:
                                moving = probs[:, 4 * SEQ + j * P:4 * SEQ + (j + 1) * P]
                                out = half[32 * j:32 * j + 32, P:2 * P]
                            last = pe.matmul(out, v.v[0:keys, k, 4 * g + j, :], moving, start=k == 0,
                                             stop=k == 1 or a == "ca")
                    last.then_inc(v.probs_used.sem, 1)
                elif what[0] == "turned":
                    b = what[2]
                    pe.wait_ge(v.heads_ready.sem, v.heads_ready.value(seq, (a, b)))
                    bank = take_bank(v, seq, what)
                    for u in range(QT):
                        for g in range(2):
                            last = pe.transpose(bank[:, (u * 2 + g) * P:(u * 2 + g + 1) * P],
                                                v.heads[:, g, u * P:(u + 1) * P], ident[:, :])
                    last.then_inc(v.ring_ready.sem, 1)
                elif what[0] == "o_proj":
                    w = f"{a}_o"
                    split_ready(v, seq, "o_t", a)
                    o = [x[:, 0:2 * SEQ].rearrange("p (k n) -> p k n", k=2) for x in (v.big_hi, v.big_lo)]
                    bank = take_bank(v, seq, what)
                    for u in range(QT):
                        last = product(bank[:, u * D:(u + 1) * D], columns(o, u * P, P),
                                       columns((w_hi[w], w_lo[w]), 0, D))
                    last.then_inc(v.ring_ready.sem, 1)
                elif what[0] == "up":
                    if a == 0:
                        split_ready(v, seq, "normal_t", ffn_ln)
                    bank = take_bank(v, seq, what)
                    for i in range(2):
                        last = product(bank[:, i * SEQ:(i + 1) * SEQ], columns((w1_hi, w1_lo), (2 * a + i) * P, P),
                                       columns(ht, 0, SEQ))
                    last.then_inc(v.ring_ready.sem, 1)
                elif what[0] == "down":
                    if a == 0:
                        take_sum(v, seq, ("down", 3))
                    split_ready(v, seq, "up", a)
                    hidden = [x[:, 2 * SEQ * (a % 2):2 * SEQ * (a % 2 + 1)].rearrange("p (k n) -> p k n", k=2)
                              for x in (v.big_hi, v.big_lo)]
                    for u in range(QT):
                        last = product(v.acc[:, u * D:(u + 1) * D], columns(hidden, u * P, P),
                                       [[x[:, 2 * a + k, :] for k in range(2)] for x in (w2_hi, w2_lo)],
                                       start=a == 0 and u == 0, stop=a == 3 and u == 1)
                    if a == 3:
                        last.then_inc(v.down_ready.sem, 1)

            in_both_slots(pe, step)


def program(nc, a):
    x = a["x"].rearrange("b n d -> (b n) d")
    ctx = a["ctx_1024"].rearrange("b n d -> (b n) d")
    mask = a["mask_BxSxS2_bk0"].rearrange("b n d -> (b n) d")
    out = a["out"].rearrange("b n d -> (b n) d")
    middle = nc.dram_tensor("middle", [BATCH * SEQ, D], F32).ap()
    l0, l1 = "L0_xattn_", "L1_xattn_"
    w0 = {f"{p}_{n}": a[f"{l0}{p}_w{n}"] for p in ("sa", "ca") for n in "qkvo"}
    w0.update(w1=a[l0 + "ffn_w1"], w2=a[l0 + "ffn_w2"])
    v0 = {f"{n}_{p}": a[f"{l0}{n}_{p}"] for n in ("ln1", "ln2", "ln3") for p in "gb"}
    v0.update(b1=a[l0 + "ffn_b1"], b2=a[l0 + "ffn_b2"])
    layer(nc, 0, x, ctx, None, middle, w0, v0)
    w1 = dict(ca_q=a[l1 + "q_w"], ca_k=a[l1 + "kv_w"][:, 0:D], ca_v=a[l1 + "kv_w"][:, D:2 * D],
              ca_o=a[l1 + "proj_w"], w1=a[l1 + "fc1_w"], w2=a[l1 + "fc2_w"])
    v1 = {f"{n}_{p}": a[f"{l1}{n}_{'w' if p == 'g' else 'b'}"] for n in ("cn", "qn", "n2") for p in "gb"}
    v1.update(b1=a[l1 + "fc1_b"], b2=a[l1 + "fc2_b"], proj_b=a[l1 + "proj_b"])
    layer(nc, 1, middle, ctx, mask, out, w1, v1)


def kernel(**inputs):
    import numpy as _np
    import concourse.bacc as _bacc
    from concourse import mybir as _mybir
    from concourse.bass_utils import run_bass_kernel_spmd as _run

    nc = _bacc.Bacc("TRN2", target_bir_lowering=False, num_devices=1)
    arrays, aps = {}, {}
    for name, value in inputs.items():
        a = _np.ascontiguousarray(value)
        arrays[f"in_{name}"] = a
        aps[name] = nc.dram_tensor(f"in_{name}", a.shape, _mybir.dt.from_np(a.dtype), kind="ExternalInput").ap()
    aps["out"] = nc.dram_tensor("out_0", (BATCH, SEQ, D), F32, kind="ExternalOutput").ap()
    program(nc, aps)
    r = _run(nc, [arrays], core_ids=[0])
    return r.results[0]["out_0"]
```

```python
import concourse.bass as bass
from concourse import mybir
from contextlib import ExitStack

F32 = mybir.dt.float32
F32R = mybir.dt.float32r
U8 = mybir.dt.uint8
ACT = mybir.ActivationFunctionType
ALU = mybir.AluOpType
AX = mybir.AxisListType

P = 128
BATCH = 64
SEQ = 256
CTX = 120
D = 256
FF = 1024
HEADS = 16
DK = D // HEADS
KT = D // P
QT = SEQ // P
PAIRS = HEADS // 2
PRODUCT_ROWS = 6 * DK
SCORE_ROWS = PRODUCT_ROWS + 2
GROUPS = 4
SLOTS = 2
PER_SLOT = BATCH // SLOTS
EPS = 1e-5
MASKED = -(2.0 ** 100)
CHUNK = 512
RING = 3
FRING = 2
PRING = 2


def head_place(h):
    t, g = divmod(h, 8)
    return (g % 4) * 2 + t, g // 4


class Signal:

    def __init__(self, sem, events, step=1):
        self.sem, self.step, self.places = sem, step, {key: n for n, key in enumerate(events)}

    def start(self, engine, prepared=0):
        if len(self.places) > prepared:
            engine.sem_inc(self.sem, self.step * (len(self.places) - prepared))

    def value(self, seq, key, back=0):
        n = len(self.places)
        return seq.count(n * self.step, (n * (1 - back) + self.places[key] + 1) * self.step)


def ring_before(n, total, size):
    if n >= size:
        return n - size, 0
    last = total - 1 - (total - 1 - n) % size
    return last, 1


CUT = [("max", "ca", 7), ("prefetch",)]
RUNS = [
    [1, 2, 1, 6, 1, 3, 1, 1, 2, 1, 7, 1, 1, 2, 2, 3, 4, 5, 1, 1, 1, 2, 1, 3, 4, 2, 3, 1, 2, 1, 2, 1, 3, 1, 3, 1,
     3, 1, 1, 3, 1, 2, 1, 1],
    [3, 3, 3, 3, 1, 2, 2, 1, 11, 1, 5, 6, 1, 2, 1, 1, 1, 1, 1, 1, 1, 1, 1, 1, 1, 1, 1],
]


def merge(second, first, runs):
    order, at, ahead = [], [0, 0], True
    for run in runs:
        steps, n = (second, 0) if ahead else (first, 1)
        order += [(ahead, step) for step in steps[at[n]:at[n] + run]]
        at[n] += run
        ahead = not ahead
    assert at == [len(second), len(first)]
    return order


class Counts:

    def __init__(self, engine, turn, scratch):
        self.engine, self.turn, self.scratch, self.bases, self.n = engine, turn, scratch, {}, 0

    def value(self, factor, constant):
        if isinstance(self.turn, int):
            assert self.turn * factor + constant > 0
            return self.turn * factor + constant
        base = self.bases[factor]
        self.n = (self.n + 1) % len(self.scratch)
        self.engine.reg_add(self.scratch[self.n], base, constant)
        return self.scratch[self.n]


class Seq:

    def __init__(self, counts, ahead=0):
        self.counts, self.ahead = counts, ahead

    def count(self, factor, constant):
        return self.counts.value(factor, self.ahead * factor + constant)

    def place(self, s):
        return self.counts.turn * SLOTS + (self.ahead * SLOTS + s)

    def next(self):
        return Seq(self.counts, self.ahead + 1)


class Slot:
    pass


def layer(nc, which, x_in, ctx_in, mask_in, x_out, weights, vectors):
    first = which == 0
    attentions = ["sa", "ca"] if first else ["ca"]
    masked = not first
    ffn_ln = "ln3" if first else "n2"
    ln_of = {"sa": "ln1", "ca": "ln2" if first else "qn"}

    def max_jobs(a):
        return 12 if a == "sa" else 8

    def score_jobs(a):
        return 3 if a == "sa" else 2

    def normalise(ln):
        return [("stats", ln), ("normal", ln), ("normal_t", ln), ("split", "normal_t", ln)]

    def projections(a):
        return [("k", a), ("split", "k", a), ("q", a), ("split", "q", a), ("v", a)]

    def attention(a):
        steps = [("max", a, n) for n in range(max_jobs(a))]
        steps += [("c", a)]
        score = [("scores", a, g) for g in range(GROUPS)]
        weighted = [("weighted", a, g) for g in range(GROUPS)]
        steps += [score[0], score[1], weighted[0], score[2], weighted[1], ("heads", a, 0), score[3],
                  weighted[2], ("turned", a, 0), weighted[3], ("heads", a, 1), ("turned", a, 1)]
        steps += [("o_t", a), ("split", "o_t", a), ("o_proj", a)]
        return steps

    up = [[("up", i), ("split", "up", i)] for i in range(4)]
    down = [[("down", i)] for i in range(4)]
    if first:
        k_ca, q_ca, v_ca = (lambda p: (p[0:2], p[2:4], p[4:5]))(projections("ca"))
        sa = attention("sa")
        o_t = sa.index(("o_t", "sa"))
        prepare = [[("stats", "ln1")], [("normal", "ln1")], [("context",), ("normal_t", "ln1")],
                   [("split", "context"), ("split", "normal_t", "ln1")] + projections("sa")[:4],
                   projections("sa")[4:]]
        steps = sa[:o_t] + k_ca + sa[o_t:-1] + v_ca + sa[-1:] + normalise("ln2") + q_ca + attention("ca") + \
            [("prefetch",)] + normalise("ln3") + [("bias", "ln3")]
    else:
        prepare = [[("mask",), ("stats", "cn")], [("normal", "cn"), ("stats", "qn")],
                   [("normal_t", "cn"), ("normal", "qn"), ("bias", "qn")],
                   [("split", "normal_t", "cn"), ("normal_t", "qn"), ("split", "normal_t", "qn")] +
                   projections("ca")[:4], projections("ca")[4:]]
        steps = attention("ca") + [("prefetch",)] + normalise("n2") + [("bias", "n2")]
    steps += up[0] + up[1] + down[0] + prepare[0] + up[2] + down[1] + prepare[1] + up[3] + prepare[2] + \
        down[2] + prepare[3] + down[3] + prepare[4]
    prepare = sum(prepare, [])
    cut = steps.index(CUT[which])
    phase1, phase2 = steps[:cut], steps[cut:]
    both = merge(phase2, phase1, RUNS[which])

    def turns_ago(event, step):
        return int(event in prepare and step not in prepare)

    ring_jobs = []
    for step in steps:
        if step[0] in ("context", "normal_t", "q", "k", "v", "o_t", "up", "max", "c", "turned", "o_proj"):
            ring_jobs.append(step)
        elif step[0] == "scores":
            ring_jobs += [(*step, n) for n in range(score_jobs(step[1]))]
    split_jobs = [step[1:] for step in steps if step[0] == "split"]
    direct_jobs = [job for job in split_jobs if job[0] not in ("normal_t", "up")]
    tile_jobs = [job for job in split_jobs if job not in direct_jobs]
    tile_halves = [(*job, half) for job in tile_jobs for half in range(2)]
    groups = [step[1:] for step in steps if step[0] == "scores"]
    sums = [("heads", a, b) for a in attentions for b in range(2)] + [("down", 3)]
    lns = [step[1] for step in steps if step[0] == "stats"]
    prepared_lns = sum(step[0] == "stats" for step in prepare)
    prepared_splits = sum(step[0] == "split" for step in prepare)
    prepared_tiles = sum(step[0] == "split" and step[1:] in tile_jobs for step in prepare)

    stack = ExitStack()
    with stack:
        def sb(name, shape, dt):
            return stack.enter_context(nc.sbuf_tensor(f"L{which}_{name}", shape, dt))

        def semaphore(name):
            return stack.enter_context(nc.semaphore(f"L{which}_{name}"))

        names = [f"{a}_{n}" for a in attentions for n in "qkvo"]
        w_hi = {n: sb(f"{n}_hi", [P, KT, D], F32R) for n in names}
        w_lo = {n: sb(f"{n}_lo", [P, KT, D], F32R) for n in names}
        w1_hi, w1_lo = sb("w1_hi", [P, KT, FF], F32R), sb("w1_lo", [P, KT, FF], F32R)
        w2_hi, w2_lo = sb("w2_hi", [P, FF // P, D], F32R), sb("w2_lo", [P, FF // P, D], F32R)
        gain = {n: sb(f"{n}_gain", [P, KT], F32) for n in lns}
        shift = {n: sb(f"{n}_shift", [P, KT], F32) for n in lns}
        b1 = sb("b1", [P, FF // P], F32)
        b2 = sb("b2", [P, D], F32)
        proj_b = None if first else sb("proj_b", [P, D], F32)
        ident = sb("ident", [P, P], F32)
        ident_r = sb("ident_r", [P, P], F32R)
        causal = sb("causal", [P, P], F32R) if first else None
        minus_half = sb("minus_half", [P, QT], F32)
        ones_row = sb("ones_row", [1, SEQ], F32)
        split = sb("split", [P, SLOTS * FRING, 512], F32)
        ring = stack.enter_context(nc.psum_tensor(f"L{which}_ring", [P, SLOTS * RING, 512], F32))
        acc = stack.enter_context(nc.psum_tensor(f"L{which}_acc", [P, SLOTS, 512], F32))

        stages = SLOTS * FRING
        w_loaded = [semaphore(f"w_loaded{n}") for n in range(stages)]
        w_lead = semaphore("w_lead")
        w_split = semaphore("w_split")
        vec_loaded = semaphore("vec_loaded")
        cleared = semaphore("cleared")
        built = semaphore("built")
        ones_set = semaphore("ones_set")
        pads_set = semaphore("pads_set")
        stats_seen = semaphore("stats_seen")

        slots, multiples = [], set()
        for s in range(SLOTS):
            v = Slot()
            slots.append(v)
            v.xin = sb(f"xin{s}", [P, QT, D], F32)
            v.x = sb(f"x{s}", [P, QT, D], F32)
            v.z = sb(f"z{s}", [P, QT, D], F32)
            v.cin = sb(f"cin{s}", [CTX, D], F32)
            v.cz = None if first else sb(f"cz{s}", [CTX, D], F32)
            v.ht_hi, v.ht_lo = (sb(f"ht_{h}{s}", [P, KT, SEQ], F32R) for h in ("hi", "lo"))
            v.ct_hi, v.ct_lo = (sb(f"ct_{h}{s}", [P, KT, CTX], F32R) for h in ("hi", "lo"))
            v.big_hi, v.big_lo = (sb(f"big_{h}{s}", [P, 4 * SEQ], F32R) for h in ("hi", "lo"))
            v.v = sb(f"v{s}", [P, 2 if first else 1, HEADS, 32], F32)
            v.qs = sb(f"qs{s}", [P, PAIRS, SEQ], F32R)
            v.ks = sb(f"ks{s}", [P, PAIRS, 2, SEQ if first else CTX], F32R)
            v.neg = sb(f"neg{s}", [P, QT, P], F32)
            v.c = sb(f"c{s}", [HEADS, SEQ], F32R)
            v.probs = sb(f"probs{s}", [P, PRING, 4 * 384 if first else 4 * SEQ], F32)
            qk = v.probs[:, :, :].rearrange("p r n -> p (r n)")[:, 0:8 * SEQ].rearrange("p (i n) -> p i n", i=4)
            v.q_hi, v.q_lo, v.k_hi, v.k_lo = (qk[:, i, :].bitcast(F32R) for i in range(4))
            v.heads = sb(f"heads{s}", [P, 2, SEQ], F32)
            v.stats = sb(f"stats{s}", [P, QT, 6], F32)
            v.mv = sb(f"mv{s}", [P, QT, 2], F32)
            v.rstd = sb(f"rstd{s}", [P, QT], F32)
            v.rden = sb(f"rden{s}", [P, 2, QT, 8], F32)
            v.mask8 = None if first else sb(f"mask8{s}", [P, QT, CTX], U8)
            v.mask = None if first else sb(f"mask{s}", [P, QT, CTX], F32R)
            v.ring = ring[:, RING * s:RING * (s + 1), :]
            v.acc = acc[:, s, :]
            v.split = split[:, FRING * s:FRING * (s + 1), :]

            def signal(name, events, step=1):
                if events:
                    multiples.add(len(events) * step)
                return Signal(semaphore(f"{name}{s}"), events, step)

            halves = [(a, b) for a in attentions for b in range(2)]
            v.ring_ready = signal("ring_ready", ring_jobs)
            v.maxed = signal("maxed", [j[1:] for j in ring_jobs if j[0] == "max"])
            v.exp_done = signal("exp_done", [j[1:] for j in ring_jobs if j[0] == "scores"])
            v.f_ready = signal("f_ready", direct_jobs)
            v.tile_ready = signal("tile_ready", tile_halves)
            v.hi_ready = signal("hi_ready", tile_jobs)
            v.hi2_ready = signal("hi2_ready", tile_jobs)
            v.lo_ready = signal("lo_ready", split_jobs)
            v.lo2_ready = signal("lo2_ready", tile_jobs)
            v.v_ready = signal("v_ready", attentions[1:] + attentions[:1])
            v.c_ready = signal("c_ready", attentions)
            v.probs_used = signal("probs_used", groups)
            v.down_ready = signal("down_ready", ["ffn"])
            v.heads_ready = signal("heads_ready", halves)
            v.rden_ready = signal("rden_ready", halves)
            v.oq_ready = signal("oq_ready", halves)
            v.x_ready = signal("x_ready", [*attentions, "ffn"])
            v.stats_ready = signal("stats_ready", lns)
            v.mv_ready = signal("mv_ready", lns)
            v.eps_ready = signal("eps_ready", lns)
            v.rstd_ready = signal("rstd_ready", lns)
            v.z_ready = signal("z_ready", [(ln, u) for ln in lns for u in range(QT)])
            v.bias_ready = signal("bias_ready", [ffn_ln] if first else [ffn_ln, "qn"])
            v.mask_ready = signal("mask_ready", ["mask"] if masked else [])
            v.xin_loaded = signal("xin_loaded", ["x"], 16)
            v.cin_loaded = signal("cin_loaded", ["c"], 16)
            v.mask_loaded = signal("mask_loaded", ["m"] if masked else [], 16)
            v.q_loaded = signal("q_loaded", [(a, n) for a in attentions[1:] + attentions[:1] for n in range(3)], 16)
            v.k_loaded = signal("k_loaded", [(a, n) for a in attentions[1:] + attentions[:1] for n in range(6)], 16)
            v.c_loaded = signal("c_loaded", attentions, 16)
            v.stored = signal("stored", ["x"], 16)

        def bank_of(v, job):
            return v.ring[:, ring_jobs.index(job) % RING, :]

        def tile_of(v, job):
            return v.split[:, tile_jobs.index(job) % FRING, :]

        def reading_done(v, job):
            if job in split_jobs:
                return (v.lo_ready, job) if job in direct_jobs else (v.tile_ready, (*job, 1))
            if job == ("down", 3):
                return v.x_ready, "ffn"
            return {"v": (v.v_ready, job[1]), "max": (v.maxed, job[1:]), "c": (v.c_ready, job[1]),
                    "scores": (v.exp_done, job[1:]), "turned": (v.oq_ready, job[1:]),
                    "heads": (v.heads_ready, job[1:]), "o_proj": (v.x_ready, job[1])}[job[0]]

        def probs_of(v, group):
            return v.probs[:, groups.index(group) % PRING, :]

        def keys_of(a):
            return SEQ if a == "sa" else CTX

        def split_to(v, job):
            if job[0] == "context" or job[-1] == "cn":
                return (v.ct_hi[:, :, :].rearrange("p k n -> p (k n)"),
                        v.ct_lo[:, :, :].rearrange("p k n -> p (k n)"), KT * CTX)
            if job[0] == "normal_t":
                return (v.ht_hi[:, :, :].rearrange("p k n -> p (k n)"),
                        v.ht_lo[:, :, :].rearrange("p k n -> p (k n)"), KT * SEQ)
            if job[0] == "q":
                return v.q_hi, v.q_lo, KT * SEQ
            if job[0] == "k":
                width = KT * keys_of(job[1])
                return v.k_hi[:, 0:width], v.k_lo[:, 0:width], width
            half = 0 if job[0] == "o_t" else job[1] % 2
            width = 2 * SEQ
            at = slice(2 * SEQ * half, 2 * SEQ * (half + 1))
            return v.big_hi[:, at], v.big_lo[:, at], width

        def in_both_slots(engine, step):
            last = Seq(Counts(engine, PER_SLOT - 1, None))
            for what in prepare:
                for s in range(SLOTS):
                    step(s, Seq(Counts(engine, 0, None), -1), what)
            for what in phase1:
                step(0, Seq(Counts(engine, 0, None)), what)
            with ExitStack() as registers:
                scratch = [registers.enter_context(engine.register(f"L{which}_wait{n}")) for n in range(4)]
                bases = {k: registers.enter_context(engine.register(f"L{which}_times{k}")) for k in sorted(multiples)}
                with engine.Fori(0, PER_SLOT - 1) as turn:
                    counts = Counts(engine, turn, scratch)
                    counts.bases = bases
                    for k, register in bases.items():
                        engine.reg_mov(register, turn * k)
                    for ahead, what in both:
                        step(0 if ahead else 1, Seq(counts), what)
                    for ahead, what in both:
                        step(1 if ahead else 0, Seq(counts, 0 if ahead else 1), what)
            ending = [(0 if ahead else 1, what) for ahead, what in both] + [(1, what) for what in phase2]
            for s, what in ending:
                if what not in prepare:
                    step(s, last, what, ending=True)

        loads = []
        for n in names:
            loads.append((n, weights[n].rearrange("(k p) n -> p k n", p=P), w_hi[n], w_lo[n]))
        for k in range(KT):
            for at in range(0, FF, CHUNK):
                loads.append(("w1", weights["w1"][k * P:(k + 1) * P, at:at + CHUNK].rearrange("p (k n) -> p k n", k=1),
                              w1_hi[:, k:k + 1, at:at + CHUNK], w1_lo[:, k:k + 1, at:at + CHUNK]))
        for k in range(0, FF // P, CHUNK // D):
            rows = slice(k * P, (k + CHUNK // D) * P)
            loads.append(("w2", weights["w2"][rows, :].rearrange("(k p) n -> p k n", p=P),
                          w2_hi[:, k:k + CHUNK // D, :], w2_lo[:, k:k + CHUNK // D, :]))
        vector_loads = [(gain[n], vectors[n + "_g"]) for n in lns] + \
            [(shift[n], vectors[n + "_b"]) for n in lns] + [(b1, vectors["b1"])]
        row_loads = [(b2, vectors["b2"])] + ([] if first else [(proj_b, vectors["proj_b"])])
        all_vectors = 16 * (len(vector_loads) + len(row_loads))

        block = stack.enter_context(nc.Block())

        @block.sync
        def _(sp):
            for n, (_, src, _, _) in enumerate(loads):
                if n >= stages:
                    sp.wait_ge(w_split, n - stages + 1)
                sp.dma_start(split[:, n % stages, :].rearrange("p (k n) -> p k n", k=src.shape[1]), src)\
                    .then_inc(w_loaded[n % stages], 16)
            with nc.allow_non_contiguous_dma(reason="one value per partition, once"):
                for dst, src in vector_loads:
                    sp.dma_start(dst[:, :], src.rearrange("(k p) -> p k", p=P)).then_inc(vec_loaded, 16)
            for dst, src in row_loads:
                sp.dma_start(dst[:, :], src.rearrange("(a n) -> a n", a=1).to_broadcast([P, D]))\
                    .then_inc(vec_loaded, 16)
            sp.wait_ge(cleared, 1)
            sp.wait_ge(ones_set, 1)
            keys = SEQ if first else CTX
            for v in slots:
                for e in range(2):
                    sp.dma_start(v.ks[PRODUCT_ROWS + e:PRODUCT_ROWS + e + 1, :, e, :].bitcast(F32),
                                 ones_row[0:1, 0:keys].rearrange("a (k n) -> a k n", k=1)
                                 .to_broadcast([1, PAIRS, keys])).then_inc(pads_set, 16)
            for v in slots:
                v.q_loaded.start(sp, 3)
                v.k_loaded.start(sp, 6)
                for sig in (v.c_loaded, v.stored):
                    sig.start(sp)

            def load(s, seq, free=None):
                v = slots[s]
                token, row = seq.place(s) * SEQ, seq.place(s) * CTX
                if free:
                    token, row = sp.snap(token), sp.snap(row)
                    sp.wait_ge(*free)
                sp.dma_start(v.xin[:, :, :], x_in[bass.ds(token, SEQ), :]
                             .rearrange("(u p) d -> p u d", p=P)).then_inc(v.xin_loaded.sem, 16)
                sp.dma_start(v.cin[:, :], ctx_in[bass.ds(row, CTX), :]).then_inc(v.cin_loaded.sem, 16)
                if masked:
                    sp.dma_start(v.mask8[:, :, :], mask_in[bass.ds(token, SEQ), :]
                                 .rearrange("(u p) d -> p u d", p=P)).then_inc(v.mask_loaded.sem, 16)

            def step(s, seq, what, ending=False):
                v = slots[s]
                if what == ("prefetch",) and not ending:
                    load(s, seq.next(), (v.x_ready.sem, v.x_ready.value(seq, attentions[0])))
                elif what[0] == "split" and what[1] == "q":
                    for c, part in ((0, v.q_hi), (2, v.q_hi), (1, v.q_lo)):
                        signal = v.lo_ready if part is v.q_lo else v.f_ready
                        if c != 2:
                            sp.wait_ge(signal.sem, signal.value(seq, what[1:]))
                        sp.dma_start(v.qs[32 * c:32 * c + 32, :, :].bitcast(F32), part.bitcast(F32))\
                            .then_inc(v.q_loaded.sem, 16)
                elif what[0] == "split" and what[1] == "k":
                    n = keys_of(what[2])
                    for c, part in ((0, v.k_hi), (1, v.k_hi), (2, v.k_lo)):
                        signal = v.lo_ready if part is v.k_lo else v.f_ready
                        if c != 1:
                            sp.wait_ge(signal.sem, signal.value(seq, what[1:]))
                        for e in range(2):
                            row = 32 * c + DK * e
                            src = part[P // 2 * e:P // 2 * (e + 1), 0:KT * n]\
                                .rearrange("p (k n) -> p k n", k=KT)
                            sp.dma_start(v.ks[row:row + DK, :, e, 0:n].bitcast(F32), src.bitcast(F32))\
                                .then_inc(v.k_loaded.sem, 16)
                elif what[0] == "c":
                    sp.wait_ge(v.c_ready.sem, v.c_ready.value(seq, what[1]))
                    sp.dma_start(v.qs[PRODUCT_ROWS:SCORE_ROWS, :, :].bitcast(F32), v.c[:, :].bitcast(F32))\
                        .then_inc(v.c_loaded.sem, 16)
                elif what == ("down", 3):
                    token = sp.snap(seq.place(s) * SEQ)
                    sp.wait_ge(v.x_ready.sem, v.x_ready.value(seq, "ffn"))
                    sp.dma_start(x_out[bass.ds(token, SEQ), :]
                                 .rearrange("(u p) d -> p u d", p=P), v.x[:, :, :]).then_inc(v.stored.sem, 16)

            for s in range(SLOTS):
                load(s, Seq(Counts(sp, 0, None)))
            in_both_slots(sp, step)
            for v in slots:
                sp.wait_ge(v.stored.sem, 16 * (PER_SLOT + 1))

        @block.gpsimd
        def _(pool):
            pool.memset(ident[:, :], 0.0).then_inc(built, 1)
            pool.memset(minus_half[:, :], -0.5)
            pool.memset(ones_row[:, :], 1.0).then_inc(ones_set, 1)
            pool.wait_ge(built, 1)
            pool.affine_select(out=ident[:, :], in_=ident[:, :], compare_op=ALU.not_equal, fill=1.0,
                               base=0, pattern=[[-1, P]], channel_multiplier=1).then_inc(built, 1)
            for v in slots:
                v.lo2_ready.start(pool, prepared_tiles)
                v.rstd_ready.start(pool, prepared_lns)
                v.bias_ready.start(pool, 0 if first else 1)
            pool.wait_ge(vec_loaded, all_vectors)

            def step(s, seq, what, ending=False):
                v = slots[s]
                if what[0] == "stats":
                    rows, us = (CTX, 1) if what[1] == "cn" else (P, QT)
                    pool.wait_ge(v.eps_ready.sem, v.eps_ready.value(seq, what[1]))
                    pool.tensor_tensor(v.rstd[0:rows, 0:us], v.rstd[0:rows, 0:us], minus_half[0:rows, 0:us],
                                       ALU.pow).then_inc(v.rstd_ready.sem, 1)
                elif what[0] == "split" and what[1:] in tile_jobs:
                    hi, lo, width = split_to(v, what[1:])
                    half = slice(0, width // 2)
                    pool.wait_ge(v.hi_ready.sem, v.hi_ready.value(seq, what[1:]))
                    pool.tensor_tensor(lo[:, half], tile_of(v, what[1:])[:, half], hi[:, half].bitcast(F32),
                                       ALU.subtract).then_inc(v.lo2_ready.sem, 1)
                elif what[0] == "bias":
                    src, row = (v.x, b2) if what[1] == ffn_ln else (v.xin, proj_b)
                    pool.wait_ge(v.z_ready.sem, v.z_ready.value(seq, (what[1], QT - 1)))
                    pool.tensor_tensor(src[:, :, :], src[:, :, :],
                                       row[:, :].rearrange("p (a n) -> p a n", a=1).to_broadcast([P, QT, D]),
                                       ALU.add).then_inc(v.bias_ready.sem, 1)

            in_both_slots(pool, step)

        @block.scalar
        def _(act):
            for v in slots:
                v.f_ready.start(act, prepared_splits - prepared_tiles)
                v.tile_ready.start(act, 2 * prepared_tiles)
                v.v_ready.start(act, 1)
                for sig in (v.exp_done, v.heads_ready):
                    sig.start(act)
            act.wait_ge(vec_loaded, all_vectors)
            act.wait_ge(w_split, len(loads))
            act.wait_ge(cleared, 1)

            def step(s, seq, what, ending=False):
                v = slots[s]
                if what in direct_jobs:
                    hi, _, width = split_to(v, what)
                    act.wait_ge(v.ring_ready.sem, v.ring_ready.value(seq, what))
                    act.activation(hi, bank_of(v, what)[:, 0:width], ACT.Copy).then_inc(v.f_ready.sem, 1)
                elif what in tile_jobs:
                    bank, tile, width = bank_of(v, what), tile_of(v, what), split_to(v, what)[2]
                    act.wait_ge(v.ring_ready.sem, v.ring_ready.value(seq, what))
                    before, back = ring_before(tile_jobs.index(what), len(tile_jobs), FRING)
                    for lo in (v.lo_ready, v.lo2_ready):
                        act.wait_ge(lo.sem, lo.value(seq, tile_jobs[before], back))
                    half = width // 2
                    for m in range(2):
                        at = slice(m * half, (m + 1) * half)
                        if what[0] == "normal_t":
                            last = act.activation(tile[:, at], bank[:, at], ACT.Identity,
                                                  bias=shift[what[1]][:, m:m + 1], scale=gain[what[1]][:, m:m + 1])
                        else:
                            column = 2 * what[1] + m
                            last = act.activation(tile[:, at], bank[:, at], ACT.Relu if first else ACT.Gelu,
                                                  bias=b1[:, column:column + 1])
                        last.then_inc(v.tile_ready.sem, 1)
                elif what[0] == "v":
                    act.wait_ge(v.ring_ready.sem, v.ring_ready.value(seq, what))
                    rows, tiles = (P, 2) if what[1] == "sa" else (CTX, 1)
                    for k in range(tiles):
                        last = act.activation(
                            v.v[0:rows, k, :, 0:DK],
                            bank_of(v, what)[0:rows, k * D:(k + 1) * D].rearrange("p (h d) -> p h d", d=DK), ACT.Copy)
                    last.then_inc(v.v_ready.sem, 1)
                elif what[0] == "scores":
                    a, g = what[1:]
                    rows = P if a == "sa" else CTX
                    before, back = ring_before(groups.index((a, g)), len(groups), PRING)
                    act.wait_ge(v.probs_used.sem, v.probs_used.value(seq, groups[before], back))
                    for n in range(score_jobs(a)):
                        act.wait_ge(v.ring_ready.sem, v.ring_ready.value(seq, (*what, n)))
                        act.activation(probs_of(v, (a, g))[0:rows, 512 * n:512 * n + 512],
                                       bank_of(v, (*what, n))[0:rows, :], ACT.Exp, scale=DK ** -0.5).then_inc(v.exp_done.sem, 1)
                elif what[0] == "heads":
                    act.wait_ge(v.probs_used.sem, v.probs_used.value(seq, (what[1], 2 * what[2] + 1)))
                    act.activation(v.heads[:, :, :].rearrange("p g n -> p (g n)"), v.acc, ACT.Copy)\
                        .then_inc(v.heads_ready.sem, 1)

            in_both_slots(act, step)

        @block.vector
        def _(dve):
            for v in slots:
                dve.memset(v.qs[:, :, :].bitcast(F32), 0.0)
                dve.memset(v.ks[:, :, :, :].bitcast(F32), 0.0)
                dve.memset(v.v[:, :, :, DK:32], 0.0)
                last = dve.memset(v.neg[:, :, :], 0.0)
            last.then_inc(w_lead, 1)
            dve.wait_ge(w_lead, 1)
            for v in slots:
                last = dve.memset(v.v[:, :, :, DK:DK + 1], 1.0)
            last.then_inc(cleared, 1)
            for n, (name, _, hi, lo) in enumerate(loads):
                dve.wait_ge(w_loaded[n % stages], 16 * (n // stages + 1))
                src = split[:, n % stages, :]
                hi, lo = (x[:, :, :].rearrange("p k n -> p (k n)") for x in (hi, lo))
                if name[-2:] in ("_q", "_k"):
                    src = src.rearrange("p (k j d) -> p k d j", k=2 * KT * KT, d=DK)
                    hi, lo = (x.rearrange("p (k d j) -> p k d j", k=2 * KT * KT, d=DK) for x in (hi, lo))
                dve.tensor_copy(hi, src).then_inc(w_lead, 1)
                dve.wait_ge(w_lead, n + 2)
                dve.tensor_tensor(lo, src, hi.bitcast(F32), ALU.subtract).then_inc(w_split, 1)
            dve.wait_ge(built, 2)
            dve.tensor_copy(ident_r[:, :], ident[:, :]).then_inc(built, 1)
            if first:
                later = slots[0].z[:, 0, 0:P]
                dve.tensor_tensor_scan(later, ident[:, :], ident[:, :], 0.0, ALU.max, ALU.max).then_inc(built, 1)
                dve.wait_ge(built, 4)
                dve.tensor_tensor(later, later, ident[:, :], ALU.subtract).then_inc(built, 1)
                dve.wait_ge(built, 5)
                dve.tensor_scalar(causal[:, :], later, MASKED, None, ALU.mult).then_inc(built, 1)
            for v in slots:
                v.hi_ready.start(dve, prepared_tiles)
                v.hi2_ready.start(dve, prepared_tiles)
                v.lo_ready.start(dve, prepared_splits)
                for sig in (v.stats_ready, v.mv_ready, v.eps_ready):
                    sig.start(dve, prepared_lns)
                v.z_ready.start(dve, QT * prepared_lns)
                for sig in (v.maxed, v.c_ready, v.rden_ready, v.oq_ready, v.x_ready):
                    sig.start(dve)

            def source(v, ln):
                if ln == "cn":
                    return v.cin[:, :].rearrange("p (u d) -> p u d", u=1)
                return v.xin if ln in ("ln1", "qn") else v.x

            def step(s, seq, what, ending=False):
                v = slots[s]
                if what[0] == "stats":
                    ln = what[1]
                    rows, us = (CTX, 1) if ln == "cn" else (P, QT)
                    if ln == "cn":
                        dve.wait_ge(v.cin_loaded.sem, v.cin_loaded.value(seq, "c"))
                    elif ln in ("ln1", "qn"):
                        dve.wait_ge(v.xin_loaded.sem, v.xin_loaded.value(seq, "x"))
                    else:
                        dve.wait_ge(v.x_ready.sem, v.x_ready.value(seq, "sa" if ln == "ln2" else "ca"))
                    for u in range(us):
                        last = dve.bn_stats(v.stats[0:rows, u, :], source(v, ln)[:, u, :])
                    last.then_inc(v.stats_ready.sem, 1)
                    dve.wait_ge(v.stats_ready.sem, v.stats_ready.value(seq, ln))
                    dve.sem_inc(stats_seen, 1)
                    for u in range(us):
                        last = dve.bn_aggr(v.mv[0:rows, u, :], v.stats[0:rows, u, :])
                    last.then_inc(v.mv_ready.sem, 1)
                    dve.wait_ge(v.mv_ready.sem, v.mv_ready.value(seq, ln))
                    dve.tensor_scalar(v.rstd[0:rows, 0:us], v.mv[0:rows, 0:us, 1], EPS, None, ALU.add)\
                        .then_inc(v.eps_ready.sem, 1)
                elif what[0] == "mask":
                    dve.wait_ge(v.mask_loaded.sem, v.mask_loaded.value(seq, "m"))
                    dve.tensor_scalar(v.mask[:, :, :], v.mask8[:, :, :], MASKED, None, ALU.mult)\
                        .then_inc(v.mask_ready.sem, 1)
                elif what[0] == "normal":
                    ln = what[1]
                    rows, us = (CTX, 1) if ln == "cn" else (P, QT)
                    dst = v.cz[:, :].rearrange("p (u d) -> p u d", u=1) if ln == "cn" else v.z
                    dve.wait_ge(v.rstd_ready.sem, v.rstd_ready.value(seq, ln))
                    for u in range(us):
                        dve.tensor_scalar(dst[:, u, :], source(v, ln)[:, u, :], v.mv[0:rows, u, 0:1],
                                          v.rstd[0:rows, u:u + 1], ALU.subtract, ALU.mult)\
                            .then_inc(v.z_ready.sem, QT // us)
                elif what[0] == "split":
                    job = what[1:]
                    hi, lo, width = split_to(v, job)
                    if job in direct_jobs:
                        dve.wait_ge(v.f_ready.sem, v.f_ready.value(seq, job))
                        dve.tensor_tensor(lo, bank_of(v, job)[:, 0:width], hi.bitcast(F32), ALU.subtract)\
                            .then_inc(v.lo_ready.sem, 1)
                    else:
                        tile, half, rest = tile_of(v, job), slice(0, width // 2), slice(width // 2, width)
                        dve.wait_ge(v.tile_ready.sem, v.tile_ready.value(seq, (*job, 0)))
                        dve.tensor_copy(hi[:, half], tile[:, half]).then_inc(v.hi_ready.sem, 1)
                        dve.wait_ge(v.tile_ready.sem, v.tile_ready.value(seq, (*job, 1)))
                        dve.tensor_copy(hi[:, rest], tile[:, rest]).then_inc(v.hi2_ready.sem, 1)
                        dve.wait_ge(v.hi2_ready.sem, v.hi2_ready.value(seq, job))
                        dve.tensor_tensor(lo[:, rest], tile[:, rest], hi[:, rest].bitcast(F32), ALU.subtract)\
                            .then_inc(v.lo_ready.sem, 1)
                elif what[0] == "max":
                    a, n = what[1:]
                    dve.wait_ge(v.ring_ready.sem, v.ring_ready.value(seq, what))
                    neg = v.neg[:, :, 0:HEADS].rearrange("p u (e r) -> p u r e", e=2)
                    if a == "ca":
                        out = neg[:, :, n, :]
                        scores = bank_of(v, what)[:, 0:QT * 2 * CTX].rearrange("p (u e k) -> p u e k", u=QT, e=2)
                    elif n < PAIRS:
                        out = neg[:, 1, n, :]
                        scores = bank_of(v, what).rearrange("p (e k) -> p e k", e=2)
                    else:
                        out = neg[:, 0, 2 * (n - PAIRS):2 * (n - PAIRS) + 2, :]
                        scores = bank_of(v, what).rearrange("p (r e k) -> p r e k", r=2, e=2)
                    dve.tensor_reduce(out, scores, AX.X, ALU.max, negate=True).then_inc(v.maxed.sem, 1)
                elif what[0] == "c":
                    dve.wait_ge(v.ring_ready.sem, v.ring_ready.value(seq, what))
                    dve.tensor_copy(v.c[:, :], bank_of(v, what)[0:HEADS, 0:SEQ]).then_inc(v.c_ready.sem, 1)
                elif what[0] == "turned":
                    a, b = what[1:]
                    dve.wait_ge(v.ring_ready.sem, v.ring_ready.value(seq, what))
                    o = bank_of(v, what).rearrange("p (u h c) -> p u h c", u=QT, c=32)
                    dve.reciprocal(v.rden[:, b, :, :], o[:, :, :, DK]).then_inc(v.rden_ready.sem, 1)
                    dve.wait_ge(v.rden_ready.sem, v.rden_ready.value(seq, (a, b)))
                    for u in range(QT):
                        last = dve.tensor_tensor(
                            v.z[:, u, b * P:(b + 1) * P].rearrange("p (h d) -> p h d", d=DK), o[:, u, :, 0:DK],
                            v.rden[:, b, u, :].rearrange("p (h d) -> p h d", d=1).to_broadcast([P, 8, DK]), ALU.mult)
                    last.then_inc(v.oq_ready.sem, 1)
                elif what[0] == "o_proj":
                    a = what[1]
                    src = v.xin if a == attentions[0] else v.x
                    if a == attentions[0]:
                        dve.wait_ge(v.stored.sem, v.stored.value(seq, "x", 1))
                    if masked:
                        dve.wait_ge(v.bias_ready.sem, v.bias_ready.value(seq, "qn", turns_ago(("bias", "qn"), what)))
                    dve.wait_ge(v.ring_ready.sem, v.ring_ready.value(seq, what))
                    dve.tensor_tensor(v.x[:, :, :].rearrange("p u d -> p (u d)"), bank_of(v, what),
                                      src[:, :, :].rearrange("p u d -> p (u d)"), ALU.add).then_inc(v.x_ready.sem, 1)
                elif what == ("down", 3):
                    dve.wait_ge(v.bias_ready.sem, v.bias_ready.value(seq, ffn_ln))
                    dve.wait_ge(v.down_ready.sem, v.down_ready.value(seq, "ffn"))
                    x = v.x[:, :, :].rearrange("p u d -> p (u d)")
                    dve.tensor_tensor(x, v.acc, x, ALU.add).then_inc(v.x_ready.sem, 1)

            in_both_slots(dve, step)

        @block.tensor
        def _(pe):
            for v in slots:
                v.ring_ready.start(pe, prepared_splits + 1)
                for sig in (v.probs_used, v.down_ready):
                    sig.start(pe)
            pe.wait_ge(w_split, len(loads))
            pe.wait_ge(built, 6 if first else 3)
            pe.wait_ge(pads_set, 16 * 2 * SLOTS)

            def take_bank(v, seq, job):
                before, back = ring_before(ring_jobs.index(job), len(ring_jobs), RING)
                done, event = reading_done(v, ring_jobs[before])
                pe.wait_ge(done.sem, done.value(seq, event, back))
                return bank_of(v, job)

            def take_sum(v, seq, key):
                before, back = ring_before(sums.index(key), len(sums), 1)
                done, event = reading_done(v, sums[before])
                pe.wait_ge(done.sem, done.value(seq, event, back))

            def product(out, stationary, moving, start=True, stop=True):
                tiles = len(stationary[0])
                for k in range(tiles):
                    for i, (x, y) in enumerate(((0, 0), (1, 0), (0, 1))):
                        last = pe.matmul(out, stationary[x][k], moving[y][k], start=start and k == 0 and i == 0,
                                         stop=stop and k == tiles - 1 and i == 2)
                return last

            def columns(pair, at, n, tiles=KT):
                return [[x[:, k, at:at + n] for k in range(tiles)] for x in pair]

            def repeated(tile, times, n=P):
                return tile.rearrange("p (a q) -> p a q", a=1).to_broadcast([P, times, n])

            def split_ready(v, seq, step, *job):
                back = turns_ago(("split", *job), step)
                pe.wait_ge(v.lo_ready.sem, v.lo_ready.value(seq, job, back))
                if job in tile_jobs:
                    pe.wait_ge(v.lo2_ready.sem, v.lo2_ready.value(seq, job, back))

            def step(s, seq, what, ending=False):
                v = slots[s]
                a = what[1] if len(what) > 1 else None
                ht, ct = (v.ht_hi, v.ht_lo), (v.ct_hi, v.ct_lo)
                if what[0] == "context" or what == ("normal_t", "cn"):
                    if first:
                        src = v.cin
                        pe.wait_ge(v.cin_loaded.sem, v.cin_loaded.value(seq, "c"))
                    else:
                        src = v.cz
                        pe.wait_ge(v.z_ready.sem, v.z_ready.value(seq, ("cn", QT - 1)))
                    bank = take_bank(v, seq, what)
                    for k in range(KT):
                        last = pe.transpose(bank[:, k * CTX:(k + 1) * CTX], src[:, k * P:(k + 1) * P],
                                            ident[0:CTX, 0:CTX])
                    last.then_inc(v.ring_ready.sem, 1)
                elif what[0] in ("normal_t", "o_t"):
                    if what[0] == "o_t":
                        pe.wait_ge(v.oq_ready.sem, v.oq_ready.value(seq, (a, 1)))
                    bank = take_bank(v, seq, what)
                    for u in range(QT):
                        if what[0] == "normal_t":
                            pe.wait_ge(v.z_ready.sem, v.z_ready.value(seq, (a, u)))
                        for k in range(KT):
                            last = pe.transpose(bank[:, (k * QT + u) * P:(k * QT + u + 1) * P],
                                                v.z[:, u, k * P:(k + 1) * P], ident[:, :])
                    last.then_inc(v.ring_ready.sem, 1)
                elif what[0] in ("q", "k"):
                    if what[0] == "q" or a == "sa":
                        split_ready(v, seq, what, "normal_t", ln_of[a])
                    else:
                        split_ready(v, seq, what, *(("context",) if first else ("normal_t", "cn")))
                    n, tokens = (SEQ, ht) if what[0] == "q" or a == "sa" else (CTX, ct)
                    w = f"{a}_{what[0]}"
                    bank = take_bank(v, seq, what)
                    for t in range(KT):
                        last = product(bank[:, t * n:(t + 1) * n], columns((w_hi[w], w_lo[w]), t * P, P),
                                       columns(tokens, 0, n))
                    last.then_inc(v.ring_ready.sem, 1)
                elif what[0] == "v":
                    tokens, tiles, rows = (ht, 2, P) if a == "sa" else (ct, 1, CTX)
                    w = f"{a}_v"
                    bank = take_bank(v, seq, what)
                    for u in range(tiles):
                        last = product(bank[0:rows, u * D:(u + 1) * D], columns(tokens, u * P, rows),
                                       columns((w_hi[w], w_lo[w]), 0, D))
                    last.then_inc(v.ring_ready.sem, 1)
                elif what[0] == "max":
                    n = what[2]
                    qs, ks = v.qs[0:PRODUCT_ROWS, :, :], v.ks[0:PRODUCT_ROWS, :, :, :]
                    if n == 0:
                        pe.wait_ge(v.q_loaded.sem, v.q_loaded.value(seq, (a, 2), turns_ago(("split", "q", a), what)))
                        pe.wait_ge(v.k_loaded.sem, v.k_loaded.value(seq, (a, 5), turns_ago(("split", "k", a), what)))
                        if masked:
                            pe.wait_ge(v.mask_ready.sem, v.mask_ready.value(seq, "mask", turns_ago(("mask",), what)))
                    bank = take_bank(v, seq, what)
                    if a == "ca":
                        halves = [bank[:, u * 2 * CTX:(u + 1) * 2 * CTX] for u in range(QT)]
                        for u in range(QT):
                            last = pe.matmul(halves[u], qs[:, n, u * P:(u + 1) * P], ks[:, n, :, 0:CTX],
                                             start=u == 0, stop=not masked and u == 1)
                        for u in range(QT if masked else 0):
                            last = pe.matmul(halves[u], ident_r[:, :], v.mask[:, u:u + 1, :].to_broadcast([P, 2, CTX]),
                                             start=False, stop=u == 1)
                    elif n < PAIRS:
                        pe.matmul(bank, qs[:, n, P:2 * P], ks[:, n, :, :], start=True, stop=False)
                        last = pe.matmul(bank.rearrange("p (e k) -> p e k", e=2)[:, :, P:2 * P], ident_r[:, :],
                                         repeated(causal[:, :], 2), start=False, stop=True)
                    else:
                        for i in range(2):
                            pair = 2 * (n - PAIRS) + i
                            pe.matmul(bank[:, i * 2 * P:(i + 1) * 2 * P], qs[:, pair, 0:P], ks[:, pair, :, 0:P],
                                      start=i == 0, stop=False)
                        last = pe.matmul(bank, ident_r[:, :], repeated(causal[:, :], 4), start=False, stop=True)
                    last.then_inc(v.ring_ready.sem, 1)
                elif what[0] == "c":
                    pe.wait_ge(v.maxed.sem, v.maxed.value(seq, (a, max_jobs(a) - 1)))
                    bank = take_bank(v, seq, what)
                    for u in range(QT):
                        last = pe.transpose(bank[:, u * P:(u + 1) * P], v.neg[:, u, :], ident[:, :])
                    last.then_inc(v.ring_ready.sem, 1)
                elif what[0] == "scores":
                    g = what[2]
                    keys = P if a == "sa" else CTX
                    qs, ks = v.qs[0:SCORE_ROWS, :, :], v.ks[0:SCORE_ROWS, :, :, :]
                    if g == 0:
                        pe.wait_ge(v.c_loaded.sem, v.c_loaded.value(seq, a))
                    for n in range(score_jobs(a)):
                        bank = take_bank(v, seq, (*what, n))
                        if n < 2:
                            two = bank[0:keys, :].rearrange("p (i q) -> p i q", i=2)
                            for i in range(2):
                                pair, e = head_place(4 * g + 2 * n + i)
                                last = pe.matmul(two[:, i, :], ks[:, pair, e, 0:keys], qs[:, pair, :],
                                                 start=i == 0, stop=first and a == "ca" and i == 1)
                            if a == "sa":
                                last = pe.matmul(two[:, :, 0:P], causal[:, :], repeated(ident_r[:, :], 2),
                                                 start=False, stop=True)
                            elif masked:
                                for u in range(QT):
                                    last = pe.matmul(two[:, :, u * P:(u + 1) * P], v.mask[:, u, :],
                                                     repeated(ident_r[:, :], 2), start=False, stop=u == 1)
                        else:
                            for i in range(4):
                                pair, e = head_place(4 * g + i)
                                pe.matmul(bank[:, i * P:(i + 1) * P], ks[:, pair, e, P:2 * P], qs[:, pair, P:2 * P],
                                          start=i == 0, stop=False)
                            last = pe.matmul(bank, causal[:, :], repeated(ident_r[:, :], 4), start=False, stop=True)
                        last.then_inc(v.ring_ready.sem, 1)
                elif what[0] == "weighted":
                    g = what[2]
                    keys = P if a == "sa" else CTX
                    if g == 0:
                        pe.wait_ge(v.v_ready.sem, v.v_ready.value(seq, a, turns_ago(("v", a), what)))
                    if g % 2 == 0:
                        take_sum(v, seq, ("heads", a, g // 2))
                    pe.wait_ge(v.exp_done.sem, v.exp_done.value(seq, (a, g, score_jobs(a) - 1)))
                    half = v.acc[:, (g % 2) * SEQ:(g % 2 + 1) * SEQ]
                    probs = probs_of(v, (a, g))
                    for k in range(2 if a == "sa" else 1):
                        for j in range(4):
                            if k == 0:
                                moving, out = probs[0:keys, j * SEQ:(j + 1) * SEQ], half[32 * j:32 * j + 32, :]
                            else:
                                moving = probs[:, 4 * SEQ + j * P:4 * SEQ + (j + 1) * P]
                                out = half[32 * j:32 * j + 32, P:2 * P]
                            last = pe.matmul(out, v.v[0:keys, k, 4 * g + j, :], moving, start=k == 0,
                                             stop=k == 1 or a == "ca")
                    last.then_inc(v.probs_used.sem, 1)
                elif what[0] == "turned":
                    b = what[2]
                    pe.wait_ge(v.heads_ready.sem, v.heads_ready.value(seq, (a, b)))
                    bank = take_bank(v, seq, what)
                    for u in range(QT):
                        for g in range(2):
                            last = pe.transpose(bank[:, (u * 2 + g) * P:(u * 2 + g + 1) * P],
                                                v.heads[:, g, u * P:(u + 1) * P], ident[:, :])
                    last.then_inc(v.ring_ready.sem, 1)
                elif what[0] == "o_proj":
                    w = f"{a}_o"
                    split_ready(v, seq, what, "o_t", a)
                    o = [x[:, 0:2 * SEQ].rearrange("p (k n) -> p k n", k=2) for x in (v.big_hi, v.big_lo)]
                    bank = take_bank(v, seq, what)
                    for u in range(QT):
                        last = product(bank[:, u * D:(u + 1) * D], columns(o, u * P, P),
                                       columns((w_hi[w], w_lo[w]), 0, D))
                    last.then_inc(v.ring_ready.sem, 1)
                elif what[0] == "up":
                    if a == 0:
                        split_ready(v, seq, what, "normal_t", ffn_ln)
                    bank = take_bank(v, seq, what)
                    for i in range(2):
                        last = product(bank[:, i * SEQ:(i + 1) * SEQ], columns((w1_hi, w1_lo), (2 * a + i) * P, P),
                                       columns(ht, 0, SEQ))
                    last.then_inc(v.ring_ready.sem, 1)
                elif what[0] == "down":
                    if a == 0:
                        take_sum(v, seq, ("down", 3))
                    split_ready(v, seq, what, "up", a)
                    hidden = [x[:, 2 * SEQ * (a % 2):2 * SEQ * (a % 2 + 1)].rearrange("p (k n) -> p k n", k=2)
                              for x in (v.big_hi, v.big_lo)]
                    for u in range(QT):
                        last = product(v.acc[:, u * D:(u + 1) * D], columns(hidden, u * P, P),
                                       [[x[:, 2 * a + k, :] for k in range(2)] for x in (w2_hi, w2_lo)],
                                       start=a == 0 and u == 0, stop=a == 3 and u == 1)
                    if a == 3:
                        last.then_inc(v.down_ready.sem, 1)

            in_both_slots(pe, step)


def program(nc, a):
    x = a["x"].rearrange("b n d -> (b n) d")
    ctx = a["ctx_1024"].rearrange("b n d -> (b n) d")
    mask = a["mask_BxSxS2_bk0"].rearrange("b n d -> (b n) d")
    out = a["out"].rearrange("b n d -> (b n) d")
    middle = nc.dram_tensor("middle", [BATCH * SEQ, D], F32).ap()
    l0, l1 = "L0_xattn_", "L1_xattn_"
    w0 = {f"{p}_{n}": a[f"{l0}{p}_w{n}"] for p in ("sa", "ca") for n in "qkvo"}
    w0.update(w1=a[l0 + "ffn_w1"], w2=a[l0 + "ffn_w2"])
    v0 = {f"{n}_{p}": a[f"{l0}{n}_{p}"] for n in ("ln1", "ln2", "ln3") for p in "gb"}
    v0.update(b1=a[l0 + "ffn_b1"], b2=a[l0 + "ffn_b2"])
    layer(nc, 0, x, ctx, None, middle, w0, v0)
    w1 = dict(ca_q=a[l1 + "q_w"], ca_k=a[l1 + "kv_w"][:, 0:D], ca_v=a[l1 + "kv_w"][:, D:2 * D],
              ca_o=a[l1 + "proj_w"], w1=a[l1 + "fc1_w"], w2=a[l1 + "fc2_w"])
    v1 = {f"{n}_{p}": a[f"{l1}{n}_{'w' if p == 'g' else 'b'}"] for n in ("cn", "qn", "n2") for p in "gb"}
    v1.update(b1=a[l1 + "fc1_b"], b2=a[l1 + "fc2_b"], proj_b=a[l1 + "proj_b"])
    layer(nc, 1, middle, ctx, mask, out, w1, v1)


def kernel(**inputs):
    import numpy as _np
    import concourse.bacc as _bacc
    from concourse import mybir as _mybir
    from concourse.bass_utils import run_bass_kernel_spmd as _run

    nc = _bacc.Bacc("TRN2", target_bir_lowering=False, num_devices=1)
    arrays, aps = {}, {}
    for name, value in inputs.items():
        a = _np.ascontiguousarray(value)
        arrays[f"in_{name}"] = a
        aps[name] = nc.dram_tensor(f"in_{name}", a.shape, _mybir.dt.from_np(a.dtype), kind="ExternalInput").ap()
    aps["out"] = nc.dram_tensor("out_0", (BATCH, SEQ, D), F32, kind="ExternalOutput").ap()
    program(nc, aps)
    r = _run(nc, [arrays], core_ids=[0])
    return r.results[0]["out_0"]
```
